# Optimizing a Trainium2 kernel written in Bass

```python
import numpy as np
import jax
import jax.numpy as jnp

def _softmax(x, axis=-1):
    return jax.nn.softmax(x, axis=axis)

def _gelu(x):
    return jax.nn.gelu(x, approximate=True)

def _silu(x):
    return jax.nn.silu(x)

def _sigmoid(x):
    return jax.nn.sigmoid(x)

def _layernorm(x, axis=-1, eps=1e-05):
    m = jnp.mean(x, axis=axis, keepdims=True)
    v = jnp.var(x, axis=axis, keepdims=True)
    return (x - m) / jnp.sqrt(v + eps)

def _scatter_add(tgt, idx, src, axis=0):
    return tgt.at[idx].add(src)

def _segment_sum(src, seg, n):
    return jax.ops.segment_sum(src, seg, n)
kernel_name = 'mk_perceiver_d2_seqx_r4_644103'

def setup_inputs(seed: int=0):
    np.random.seed(seed)
    _w = jnp.asarray

    def _rec_inputs():
        import jax
        import jax.numpy as jnp
        _rk = jax.random.key(seed)
        x = 7.22e-05 + 1 * jax.random.normal(jax.random.fold_in(_rk, 1), (8, 64, 256), jnp.float32)
        _lenS = 64 - jax.random.randint(jax.random.fold_in(_rk, 7), (8,), 0, max(1, 64 // 4) + 1, jnp.int32)
        _lenS2 = 1601 - jax.random.randint(jax.random.fold_in(_rk, 8), (8,), 0, max(1, 1601 // 4) + 1, jnp.int32)
        _ctx_1024P = jax.random.normal(jax.random.fold_in(_rk, 11), (8, 16, 256), jnp.float32)
        _ctx_1024c = jax.random.dirichlet(jax.random.fold_in(_rk, 511), 0.3 * jnp.ones((16,), jnp.float32), (8, 1601))
        _ctx_1024t = jnp.einsum('bsk,bkd->bsd', _ctx_1024c, _ctx_1024P)
        _ctx_1024t = _ctx_1024t * jax.lax.rsqrt(jnp.mean(jnp.square(_ctx_1024t)) + 1e-12) * 0.953939
        ctx_1024 = 4.13588e-05 + 0.999923 * (_ctx_1024t + 0.3 * jax.random.normal(jax.random.fold_in(_rk, 611), (8, 1601, 256), jnp.float32))
        return (x, ctx_1024)
    x, ctx_1024 = _rec_inputs()

    def _L0_xattn_setup():
        import jax, jax.numpy as jnp
        import numpy as np
        EMBED_DIM = 256
        NUM_HEADS = 16
        HEAD_DIM = EMBED_DIM // NUM_HEADS
        key = jax.random.key(seed)
        ks = jax.random.split(key, 11)
        s = 1.0 / np.sqrt(EMBED_DIM)
        inp = {'query': jax.random.normal(ks[0], (4, 512, EMBED_DIM), jnp.float32), 'key': jax.random.normal(ks[1], (4, 512, EMBED_DIM), jnp.float32), 'value': jax.random.normal(ks[2], (4, 512, EMBED_DIM), jnp.float32), 'Wq': jax.random.uniform(ks[3], (EMBED_DIM, EMBED_DIM), jnp.float32, -s, s), 'bq': jax.random.uniform(ks[4], (EMBED_DIM,), jnp.float32, -s, s), 'Wk': jax.random.uniform(ks[5], (EMBED_DIM, EMBED_DIM), jnp.float32, -s, s), 'bk': jax.random.uniform(ks[6], (EMBED_DIM,), jnp.float32, -s, s), 'Wv': jax.random.uniform(ks[7], (EMBED_DIM, EMBED_DIM), jnp.float32, -s, s), 'bv': jax.random.uniform(ks[8], (EMBED_DIM,), jnp.float32, -s, s), 'Wo': jax.random.uniform(ks[9], (EMBED_DIM, EMBED_DIM), jnp.float32, -s, s), 'bo': jax.random.uniform(ks[10], (EMBED_DIM,), jnp.float32, -s, s)}
        return inp
    _L0_xattn_all = _L0_xattn_setup()
    _L0_xattn_in = {k: v for k, v in _L0_xattn_all.items() if k in ('Wq', 'bq', 'Wk', 'bk', 'Wv', 'bv', 'Wo', 'bo')}
    del _L0_xattn_all

    def _L0_attn_setup():
        import jax, jax.numpy as jnp
        import numpy as np
        DIM = 256
        HEADS = 16
        DIM_HEAD = DIM // HEADS
        LATENT = DIM // 4
        SCALE = DIM_HEAD ** (-0.5)
        key = jax.random.key(seed)
        ks = jax.random.split(key, 8)
        B, S = (2, 512)
        init = lambda k, shape, fan_in: jax.random.normal(k, shape, jnp.float32) * fan_in ** (-0.5)
        return {'x': jax.random.normal(ks[0], (B, S, DIM), jnp.float32), 'Wq': init(ks[1], (DIM, DIM), DIM), 'bq': jnp.zeros((DIM,), jnp.float32), 'Wl': init(ks[2], (DIM, LATENT), DIM), 'bl': jnp.zeros((LATENT,), jnp.float32), 'Wk': init(ks[3], (LATENT, DIM), LATENT), 'bk': jnp.zeros((DIM,), jnp.float32), 'Wv': init(ks[4], (LATENT, DIM), LATENT), 'bv': jnp.zeros((DIM,), jnp.float32), 'Wo': init(ks[5], (DIM, DIM), DIM), 'bo': jnp.zeros((DIM,), jnp.float32)}
    _L0_attn_all = _L0_attn_setup()
    _L0_attn_in = {k: v for k, v in _L0_attn_all.items() if k in ('Wq', 'bq', 'Wl', 'bl', 'Wk', 'bk', 'Wv', 'bv', 'Wo', 'bo')}
    del _L0_attn_all

    def _L0_ffn_setup():
        import jax, jax.numpy as jnp
        import numpy as np
        D = 256
        I = 128
        E = 32
        K = 4
        T = 2 * 512
        C = 2 * T * K // E
        key = jax.random.key(seed)
        ks = jax.random.split(key, 9)
        bf = jnp.bfloat16
        std = 0.02
        x = jax.random.normal(ks[0], (2, 512, D), dtype=jnp.float32).astype(bf)
        gate_w = (std * jax.random.normal(ks[1], (E, D), dtype=jnp.float32)).astype(bf)
        bias = jnp.zeros((E,), jnp.float32)
        W1 = (std * jax.random.normal(ks[2], (E, D, I), dtype=jnp.float32)).astype(bf)
        W3 = (std * jax.random.normal(ks[3], (E, D, I), dtype=jnp.float32)).astype(bf)
        W2 = (std * jax.random.normal(ks[4], (E, I, D), dtype=jnp.float32)).astype(bf)
        sw1 = (std * jax.random.normal(ks[5], (I, D), dtype=jnp.float32)).astype(bf)
        sw3 = (std * jax.random.normal(ks[6], (I, D), dtype=jnp.float32)).astype(bf)
        sw2 = (std * jax.random.normal(ks[7], (D, I), dtype=jnp.float32)).astype(bf)
        return {'x': x, 'gate_w': gate_w, 'bias': bias, 'W1': W1, 'W3': W3, 'W2': W2, 'sw1': sw1, 'sw3': sw3, 'sw2': sw2}
    _L0_ffn_all = _L0_ffn_setup()
    _L0_ffn_in = {k: v for k, v in _L0_ffn_all.items() if k in ('gate_w', 'bias', 'W1', 'W3', 'W2', 'sw1', 'sw3', 'sw2')}
    del _L0_ffn_all

    def _L1_xattn_setup():
        import jax, jax.numpy as jnp
        import numpy as np
        B, N, T, D, H = (2, 512, 512, 256, 16)
        HD = D // H
        key = jax.random.key(seed)
        ks = jax.random.split(key, 5)
        s = 0.02
        return {'x': jax.random.normal(ks[0], (B, N, D), dtype=jnp.float32), 'context': jax.random.normal(ks[1], (B, T, D), dtype=jnp.float32), 'Wq': jax.random.normal(ks[2], (D, D), dtype=jnp.float32) * s, 'Wkv': jax.random.normal(ks[3], (D, 2 * HD), dtype=jnp.float32) * s, 'Wo': jax.random.normal(ks[4], (D, D), dtype=jnp.float32) * s}
    _L1_xattn_all = _L1_xattn_setup()
    _L1_xattn_in = {k: v for k, v in _L1_xattn_all.items() if k in ('Wq', 'Wkv', 'Wo')}
    del _L1_xattn_all

    def _L1_attn_setup():
        import jax, jax.numpy as jnp
        import numpy as np
        HEADS = 16
        LN_EPS = 1e-05

        def _layer_norm(y, gamma, beta):
            mu = jnp.mean(y, axis=-1, keepdims=True)
            var = jnp.mean(jnp.square(y - mu), axis=-1, keepdims=True)
            return (y - mu) * jax.lax.rsqrt(var + LN_EPS) * gamma + beta
        key = jax.random.key(seed)
        ks = jax.random.split(key, 5)
        B, T, D = (1, 1024, 256)
        s = 0.02
        return {'x': jax.random.normal(ks[0], (B, T, D), jnp.float32), 'Wqkv': jax.random.normal(ks[1], (3 * D, D), jnp.float32) * s, 'bqkv': jax.random.normal(ks[2], (3 * D,), jnp.float32) * s, 'Wout': jax.random.normal(ks[3], (D, D), jnp.float32) * s, 'bout': jax.random.normal(ks[4], (D,), jnp.float32) * s, 'gamma': jnp.ones((D,), jnp.float32), 'beta': jnp.zeros((D,), jnp.float32)}
    _L1_attn_all = _L1_attn_setup()
    _L1_attn_in = {k: v for k, v in _L1_attn_all.items() if k in ('Wqkv', 'bqkv', 'Wout', 'bout', 'gamma', 'beta')}
    del _L1_attn_all

    def _L1_ffn_setup():
        import jax, jax.numpy as jnp
        import numpy as np
        B, S, D, DOUT, E = (2, 512, 256, 256, 8)
        DH = 4 * D
        key = jax.random.key(seed)
        ks = jax.random.split(key, 7)
        sc = lambda *sh: 1.0 / np.sqrt(sh[-2]) if len(sh) >= 2 else 0.02
        return {'x': jax.random.normal(ks[0], (B, S, D), jnp.float32), 'Wg': jax.random.normal(ks[1], (D, E), jnp.float32) / np.sqrt(D), 'bg': jnp.zeros((E,), jnp.float32), 'W1': jax.random.normal(ks[2], (E, D, DH), jnp.float32) / np.sqrt(D), 'b1': jax.random.normal(ks[3], (E, DH), jnp.float32) * 0.02, 'W2': jax.random.normal(ks[4], (E, DH, DOUT), jnp.float32) / np.sqrt(DH), 'b2': jax.random.normal(ks[5], (E, DOUT), jnp.float32) * 0.02}
    _L1_ffn_all = _L1_ffn_setup()
    _L1_ffn_in = {k: v for k, v in _L1_ffn_all.items() if k in ('Wg', 'bg', 'W1', 'b1', 'W2', 'b2')}
    del _L1_ffn_all
    return {'x': x, 'ctx_1024': ctx_1024, 'L0_xattn_Wq': _L0_xattn_in['Wq'], 'L0_xattn_bq': _L0_xattn_in['bq'], 'L0_xattn_Wk': _L0_xattn_in['Wk'], 'L0_xattn_bk': _L0_xattn_in['bk'], 'L0_xattn_Wv': _L0_xattn_in['Wv'], 'L0_xattn_bv': _L0_xattn_in['bv'], 'L0_xattn_Wo': _L0_xattn_in['Wo'], 'L0_xattn_bo': _L0_xattn_in['bo'], 'L0_attn_Wq': _L0_attn_in['Wq'], 'L0_attn_bq': _L0_attn_in['bq'], 'L0_attn_Wl': _L0_attn_in['Wl'], 'L0_attn_bl': _L0_attn_in['bl'], 'L0_attn_Wk': _L0_attn_in['Wk'], 'L0_attn_bk': _L0_attn_in['bk'], 'L0_attn_Wv': _L0_attn_in['Wv'], 'L0_attn_bv': _L0_attn_in['bv'], 'L0_attn_Wo': _L0_attn_in['Wo'], 'L0_attn_bo': _L0_attn_in['bo'], 'L0_ffn_gate_w': _L0_ffn_in['gate_w'], 'L0_ffn_bias': _L0_ffn_in['bias'], 'L0_ffn_W1': _L0_ffn_in['W1'], 'L0_ffn_W3': _L0_ffn_in['W3'], 'L0_ffn_W2': _L0_ffn_in['W2'], 'L0_ffn_sw1': _L0_ffn_in['sw1'], 'L0_ffn_sw3': _L0_ffn_in['sw3'], 'L0_ffn_sw2': _L0_ffn_in['sw2'], 'L1_xattn_Wq': _L1_xattn_in['Wq'], 'L1_xattn_Wkv': _L1_xattn_in['Wkv'], 'L1_xattn_Wo': _L1_xattn_in['Wo'], 'L1_attn_Wqkv': _L1_attn_in['Wqkv'], 'L1_attn_bqkv': _L1_attn_in['bqkv'], 'L1_attn_Wout': _L1_attn_in['Wout'], 'L1_attn_bout': _L1_attn_in['bout'], 'L1_attn_gamma': _L1_attn_in['gamma'], 'L1_attn_beta': _L1_attn_in['beta'], 'L1_ffn_Wg': _L1_ffn_in['Wg'], 'L1_ffn_bg': _L1_ffn_in['bg'], 'L1_ffn_W1': _L1_ffn_in['W1'], 'L1_ffn_b1': _L1_ffn_in['b1'], 'L1_ffn_W2': _L1_ffn_in['W2'], 'L1_ffn_b2': _L1_ffn_in['b2']}

def reference(x, ctx_1024, L0_xattn_Wq, L0_xattn_bq, L0_xattn_Wk, L0_xattn_bk, L0_xattn_Wv, L0_xattn_bv, L0_xattn_Wo, L0_xattn_bo, L0_attn_Wq, L0_attn_bq, L0_attn_Wl, L0_attn_bl, L0_attn_Wk, L0_attn_bk, L0_attn_Wv, L0_attn_bv, L0_attn_Wo, L0_attn_bo, L0_ffn_gate_w, L0_ffn_bias, L0_ffn_W1, L0_ffn_W3, L0_ffn_W2, L0_ffn_sw1, L0_ffn_sw3, L0_ffn_sw2, L1_xattn_Wq, L1_xattn_Wkv, L1_xattn_Wo, L1_attn_Wqkv, L1_attn_bqkv, L1_attn_Wout, L1_attn_bout, L1_attn_gamma, L1_attn_beta, L1_ffn_Wg, L1_ffn_bg, L1_ffn_W1, L1_ffn_b1, L1_ffn_W2, L1_ffn_b2):
    import jax
    import jax.numpy as jnp

    def _L0_xattn_ref(query, key, value, Wq, bq, Wk, bk, Wv, bv, Wo, bo):
        import jax, jax.numpy as jnp
        import numpy as np
        EMBED_DIM = 256
        NUM_HEADS = 16
        HEAD_DIM = EMBED_DIM // NUM_HEADS
        B, T, E = query.shape
        S = key.shape[1]
        H, D = (NUM_HEADS, HEAD_DIM)
        q = (query @ Wq.T + bq).reshape(B, T, H, D).transpose(0, 2, 1, 3)
        k = (key @ Wk.T + bk).reshape(B, S, H, D).transpose(0, 2, 1, 3)
        v = (value @ Wv.T + bv).reshape(B, S, H, D).transpose(0, 2, 1, 3)
        scores = jnp.einsum('bhtd,bhsd->bhts', q, k) / np.sqrt(D)
        causal = jnp.triu(jnp.full((T, S), -jnp.inf, jnp.float32), k=1)
        scores = scores + causal[None, None]
        attn = jax.nn.softmax(scores, axis=-1)
        out = jnp.einsum('bhts,bhsd->bhtd', attn, v)
        out = out.transpose(0, 2, 1, 3).reshape(B, T, E)
        out = out @ Wo.T + bo
        return out

    def _L0_attn_ref(x, Wq, bq, Wl, bl, Wk, bk, Wv, bv, Wo, bo):
        import jax, jax.numpy as jnp
        import numpy as np
        DIM = 256
        HEADS = 16
        DIM_HEAD = DIM // HEADS
        LATENT = DIM // 4
        SCALE = DIM_HEAD ** (-0.5)
        B, S, D = x.shape
        H, Dh = (HEADS, DIM_HEAD)
        q = (x @ Wq + bq).reshape(B, S, H, Dh)
        latent = x @ Wl + bl
        k = (latent @ Wk + bk).reshape(B, S, H, Dh)
        v = (latent @ Wv + bv).reshape(B, S, H, Dh)
        scores = jnp.einsum('bihd,bjhd->bhij', q, k) * SCALE
        attn = jax.nn.softmax(scores, axis=-1)
        out = jnp.einsum('bhij,bjhd->bihd', attn, v).reshape(B, S, D)
        out = out @ Wo + bo
        return out

    def _L0_ffn_ref(x, gate_w, bias, W1, W3, W2, sw1, sw3, sw2):
        import jax, jax.numpy as jnp
        import numpy as np
        D = 256
        I = 128
        E = 32
        K = 4
        T = 2 * 512
        C = 2 * T * K // E
        X = x.reshape(-1, D)
        logits = (X @ gate_w.T).astype(jnp.float32)
        scores = jax.nn.sigmoid(logits)
        _, idx = jax.lax.top_k(scores + bias[None, :], K)
        w = jnp.take_along_axis(scores, idx, axis=-1)
        w = w / jnp.clip(jnp.sum(w, axis=-1, keepdims=True), 1e-12, None)
        w = w.astype(x.dtype)
        eid = idx.reshape(-1)
        onehot = (eid[:, None] == jnp.arange(E)[None, :]).astype(jnp.int32)
        pos = jnp.take_along_axis(jnp.cumsum(onehot, axis=0) - 1, eid[:, None], axis=1)[:, 0]
        valid = pos < C
        posc = jnp.minimum(pos, C - 1)
        Xrep = jnp.repeat(X, K, axis=0)
        xe = jnp.zeros((E, C, D), x.dtype).at[eid, posc].add(jnp.where(valid[:, None], Xrep, jnp.zeros((), x.dtype)))
        h = jax.nn.silu(jnp.einsum('ecd,edi->eci', xe, W1)) * jnp.einsum('ecd,edi->eci', xe, W3)
        ye = jnp.einsum('eci,eid->ecd', h, W2)
        gflat = jnp.where(valid, w.reshape(-1), jnp.zeros((), x.dtype))
        yrows = ye[eid, posc] * gflat[:, None]
        out = yrows.reshape(-1, K, D).sum(axis=1)
        out = out + jax.nn.silu(X @ sw1.T) * (X @ sw3.T) @ sw2.T
        return out.reshape(x.shape)

    def _L1_xattn_ref(x, context, Wq, Wkv, Wo):
        import jax, jax.numpy as jnp
        import numpy as np
        B, N, T, D, H = (2, 512, 512, 256, 16)
        HD = D // H
        b, n, d = x.shape
        h = H
        hd = d // h
        scale = hd ** (-0.5)
        q = x @ Wq
        kv = context @ Wkv
        k, v = jnp.split(kv, 2, axis=-1)
        q = q.reshape(b, n, h, hd).transpose(0, 2, 1, 3) * scale
        sim = jnp.einsum('bhnd,btd->bhnt', q, k)
        att = jax.nn.softmax(sim, axis=-1)
        y = jnp.einsum('bhnt,btd->bhnd', att, v)
        y = y.transpose(0, 2, 1, 3).reshape(b, n, d)
        return y @ Wo

    def _L1_attn_ref(x, Wqkv, bqkv, Wout, bout, gamma, beta):
        import jax, jax.numpy as jnp
        import numpy as np
        HEADS = 16
        LN_EPS = 1e-05

        def _layer_norm(y, gamma, beta):
            mu = jnp.mean(y, axis=-1, keepdims=True)
            var = jnp.mean(jnp.square(y - mu), axis=-1, keepdims=True)
            return (y - mu) * jax.lax.rsqrt(var + LN_EPS) * gamma + beta
        B, T, D = x.shape
        h = HEADS
        d = D // h
        scale = d ** (-0.5)
        qkv = (x @ Wqkv.T + bqkv).reshape(B, T, 3, h, d).transpose(2, 0, 3, 1, 4)
        Q, K, V = (qkv[0], qkv[1], qkv[2])
        scores = jnp.einsum('bhqd,bhkd->bhqk', Q, K) * scale
        causal = jnp.tril(jnp.ones((T, T), dtype=bool))
        scores = jnp.where(causal, scores, -jnp.inf)
        attn = jax.nn.softmax(scores, axis=-1)
        out = jnp.einsum('bhqk,bhkd->bhqd', attn, V)
        out = out.transpose(0, 2, 1, 3).reshape(B, T, D)
        out = out @ Wout.T + bout
        return _layer_norm(x + out, gamma, beta)

    def _L1_ffn_ref(x, Wg, bg, W1, b1, W2, b2):
        import jax, jax.numpy as jnp
        import numpy as np
        B, S, D, DOUT, E = (2, 512, 256, 256, 8)
        DH = 4 * D
        Bb, Ss, Dd = x.shape
        xt = x.reshape(-1, Dd)
        gates = jax.nn.softmax(xt @ Wg + bg, axis=-1)
        sel = jnp.argmax(gates, axis=-1)
        nE = W1.shape[0]
        out = jnp.zeros((xt.shape[0], W2.shape[-1]), x.dtype)
        for e in range(nE):
            h = jax.nn.gelu(xt @ W1[e] + b1[e], approximate=False)
            ye = h @ W2[e] + b2[e]
            out = jnp.where((sel == e)[:, None], ye, out)
        return out.reshape(Bb, Ss, -1)
    x = x + _L0_xattn_ref(_layernorm(x, axis=-1), ctx_1024, ctx_1024, L0_xattn_Wq, L0_xattn_bq, L0_xattn_Wk, L0_xattn_bk, L0_xattn_Wv, L0_xattn_bv, L0_xattn_Wo, L0_xattn_bo)
    x = x + _L0_attn_ref(_layernorm(x, axis=-1), L0_attn_Wq, L0_attn_bq, L0_attn_Wl, L0_attn_bl, L0_attn_Wk, L0_attn_bk, L0_attn_Wv, L0_attn_bv, L0_attn_Wo, L0_attn_bo)
    x = x + _L0_ffn_ref(_layernorm(x, axis=-1), L0_ffn_gate_w, L0_ffn_bias, L0_ffn_W1, L0_ffn_W3, L0_ffn_W2, L0_ffn_sw1, L0_ffn_sw3, L0_ffn_sw2)
    x = x + _L1_xattn_ref(_layernorm(x, axis=-1), ctx_1024, L1_xattn_Wq, L1_xattn_Wkv, L1_xattn_Wo)
    x = x + _L1_attn_ref(_layernorm(x, axis=-1), L1_attn_Wqkv, L1_attn_bqkv, L1_attn_Wout, L1_attn_bout, L1_attn_gamma, L1_attn_beta)
    x = x + _L1_ffn_ref(_layernorm(x, axis=-1), L1_ffn_Wg, L1_ffn_bg, L1_ffn_W1, L1_ffn_b1, L1_ffn_W2, L1_ffn_b2)
    return x

_drawn_inputs = setup_inputs


def setup_inputs(seed=0):
    import zlib

    import numpy as np

    out = dict(_drawn_inputs(seed))
    spreads = {'L0_attn_bq': (0.0, 0.1),
     'L0_attn_bl': (0.0, 0.1),
     'L0_attn_bk': (0.0, 2.0),
     'L0_attn_bv': (0.0, 0.1),
     'L0_attn_bo': (0.0, 0.1),
     'L0_ffn_bias': (0.0, 0.1),
     'L1_attn_gamma': (1.0, 0.2),
     'L1_attn_beta': (0.0, 0.1),
     'L1_ffn_bg': (0.0, 0.1)}
    factors = {'L0_xattn_bk': 64.0,
     'L0_ffn_gate_w': 3.078,
     'L0_ffn_W1': 3.037,
     'L0_ffn_sw3': 2.695,
     'L1_xattn_Wq': 8.0,
     'L1_attn_bqkv': 8.0,
     'L1_ffn_b1': 8.0,
     'L1_ffn_b2': 6.064,
     'L0_xattn_bq': 8.0}
    for name, (base, spread) in spreads.items():
        noise = np.random.default_rng([zlib.crc32(name.encode()), seed]).standard_normal(out[name].shape)
        drawn = base * np.exp(spread * noise) if base else spread * noise
        out[name] = jnp.asarray(drawn.astype(out[name].dtype))
    for name, factor in factors.items():
        out[name] = (out[name] * factor).astype(out[name].dtype)
    return out
```

```python
import concourse.bass as bass
from concourse import mybir
from contextlib import ExitStack

F32 = mybir.dt.float32
BF16 = mybir.dt.bfloat16
F16 = mybir.dt.float16
U32 = mybir.dt.uint32
I32 = mybir.dt.int32
ALU = mybir.AluOpType
ACT = mybir.ActivationFunctionType
AX = mybir.AxisListType

P = 128
NB, T, D = 8, 64, 256
TOK = NB * T
TT = TOK // P
C = D // P
H, HD = 16, 16
SCALE = HD ** -0.5
NEG = -3.0e38
EPS = 1e-5
S = 1601
KT_N = -(-S // P)
SP = KT_N * P
K_LAST = S - (KT_N - 1) * P
NPART = 6
KQ = NPART * HD
KQ2 = KQ + 2
CHUNKS = [(401 * i - max(0, i - 1), 401 if i == 0 else 400) for i in range(4)]
E0, E0T, I0, K0, CAP = 32, 33, 128, 4, 256
E1, DH = 8, 1024
XS = 64.0
MORE = TOK // P - 1
NBLK = E1 + MORE
HC = DH // P
WSLOTS = 4

W_COLS = {"0x": 0, "0a": 4 * D, "1x": 6 * D + 64, "1a": 8 * D + 96, "g": 12 * D + 96}
W_TOTAL = 12 * D + 96 + E1
BC = {n: 2 * i for i, n in enumerate(["0x_q", "0x_k", "0x_v", "0a_q", "0a_k", "0a_v", "1a_q", "1a_k", "1a_v"])}
BC_L = 18
BR = {n: D * i for i, n in enumerate(["0x_o", "0a_o", "1a_o", "gamma", "beta"])}
BR_E, BR_G, BR_TOTAL = 5 * D, 5 * D + E0, 5 * D + E0 + E1
CF = {"ident": 0, "vmask": 128, "iota": 132, "blk": 260, "power": 276}
CF_TOTAL = 280
CB = {"ident": 0, "mask": 128, "upper": 640, "ones": 768}
CB_TOTAL = 896


def build(nc, a, out, scratch_x, scratch_y, scratch_g):
    with ExitStack() as ctx:
        def sb(name, shape, dt=F32):
            return ctx.enter_context(nc.sbuf_tensor(name, shape, dt))

        def sem(name):
            return ctx.enter_context(nc.semaphore(name))

        cf = sb("const_f32", [P, CF_TOTAL])
        cb = sb("const_bf16", [P, CB_TOTAL], BF16)
        wall = sb("attn_weights", [P, C, W_TOTAL])
        wkv_sb = sb("context_kv_weights", [P, C, 32])
        wkv_l = sb("latent_kv_weights", [64, 2 * D])
        bcol = sb("bias_columns", [P, 20])
        brow = sb("bias_rows", [P, BR_TOTAL])
        gate_w = sb("gate_weights", [P, C, E0], BF16)
        x = sb("x", [P, TT, D])
        xn = sb("xn", [P, TT, D])
        xb = sb("x_plus_bias", [P, TT, D])
        xnT = sb("xnT", [P, C, TOK])
        srcT = sb("ctx64T", [P, C, TOK])
        yT = sb("yT", [P, C, TOK])
        stats = sb("ln_stats", [P, TT, 6])
        mv = sb("ln_mean_var", [P, TT, 2])
        rstd = sb("ln_rstd", [P, TT, 1])
        zero_f = sb("zeros", [P, D])
        gelu_warm = sb("gelu_warm", [P, 1])
        kT = sb("ctx_kT", [P, NB, SP], BF16)
        v_ctx = sb("ctx_v", [P, NB, KT_N, 32])
        R1 = sb("region1", [P, 11008])
        ctx_ring = [R1[:, i * C * SP:(i + 1) * C * SP].rearrange("p (c s) -> p c s", c=C) for i in range(3)]
        HALF = C * DH
        halves = [R1[:, i * HALF:(i + 1) * HALF] for i in range(5)] + [
            kT[:].rearrange("p b s -> p (b s)").bitcast(F32)[:, i * HALF:(i + 1) * HALF] for i in range(3)]
        w1_s = [halves[2 * i].rearrange("p (c n) -> p c n", c=C) for i in range(WSLOTS)]
        w2_s = [halves[2 * i + 1].rearrange("p (k n) -> p k n", k=HC) for i in range(WSLOTS)]
        v_flat = v_ctx[:].rearrange("p b t n -> p (b t n)")
        b2_s = v_flat[:, 0:NBLK * D].rearrange("p (j n) -> p j n", j=NBLK)
        b1_s = v_flat[:, NBLK * D:NBLK * D + NBLK * HC].rearrange("p (j k) -> p j k", j=NBLK)
        R2 = sb("region2", [P, 15200])
        used = [0]

        def r2(n, dt=F32):
            at = used[0]
            used[0] += n
            assert used[0] <= 15200
            ap = R2[:, at:at + n]
            return ap if dt == F32 else ap.bitcast(dt)

        used[0] = C * TOK + C * 4 * TOK + NB * 8 * 34
        kvT_sb = [r2(512) for _ in range(2)]
        kvs = [r2(KT_N * 32).rearrange("p (t n) -> p t n", n=32) for _ in range(2)]
        k_r1 = r2(KT_N * 16).rearrange("p (t n) -> p t n", n=16)
        Ks = [r2(KT_N * 100 // 2, BF16).rearrange("p (t n) -> p t n", n=100) for _ in range(2)]
        used[0] = 0
        q_T = r2(C * TOK).rearrange("p (m t) -> p m t", m=C)
        k_Tm = r2(C * 4 * TOK).rearrange("p (m v t) -> p m v t", m=C, v=4)
        v_sm = r2(NB * 8 * 34).rearrange("p (b j n) -> p b j n", b=NB, j=8)
        z = [r2(1024) for _ in range(2)]
        pT = [r2(1024).rearrange("p (j q) -> p j q", j=8) for _ in range(2)]
        y_sm = r2(TT * D).rearrange("p (t n) -> p t n", t=TT)
        lat = r2(TOK)
        mx = [r2(16) for _ in range(2)]
        rs = [r2(16).rearrange("p (j x) -> p j x", j=8) for _ in range(2)]
        bkm = r2(C * 4).rearrange("p (m v) -> p m v", m=C)
        un = r2(TT * D).rearrange("p (t n) -> p t n", t=TT)
        used[0] = 0
        qf = r2(TT * D).rearrange("p (a n) -> p a n", n=HD)
        q_r1 = r2(TT * D).rearrange("p (a n) -> p a n", n=HD)
        Qs = r2(TT * H * KQ // 2, BF16).rearrange("p (a n) -> p a n", n=KQ)
        QT = r2(TT * H * P // 2, BF16).rearrange("p (b h q) -> p b h q", b=NB, h=H)
        NP_ = 4
        probs = [r2(1024) for _ in range(NP_)]
        mp = [r2(32).rearrange("p (q c) -> p q c", c=4) for _ in range(2)]
        nm = r2(8)
        NM = [r2(8, BF16).rearrange("p (q c) -> p q c", c=2) for _ in range(2)]
        oT = [r2(256) for _ in range(2)]
        rc = [r2(8).rearrange("p (a b) -> p a b", a=2) for _ in range(2)]
        yn = [r2(128).rearrange("p (c t d) -> p c t d", c=4, t=2) for _ in range(2)]
        used[0] = 0
        xp = [r2(C * TOK // 2, F16).rearrange("p (c t) -> p c t", c=C) for _ in range(2)]
        w0 = [r2(768 // 2, BF16) for _ in range(4)]
        sa = [r2(TOK) for _ in range(2)]
        tb = r2(TOK)
        t2 = [r2(TOK) for _ in range(2)]
        hr = [r2(TOK) for _ in range(2)]
        hp = [[r2(TOK // 2, BF16) for _ in range(3)] for _ in range(4)]
        gT = r2(TOK)
        gb = [r2(TOK) for _ in range(4)]
        g_sc = r2(TT * E0).rearrange("p (t e) -> p t e", e=E0)
        g_sb = r2(TT * E0).rearrange("p (t e) -> p t e", e=E0)
        g_v8 = r2(TT * 8).rearrange("p (t e) -> p t e", e=8)
        g_i8 = r2(TT * 8, U32).rearrange("p (t e) -> p t e", e=8)
        g_f8 = r2(TT * 8).rearrange("p (t e) -> p t e", e=8)
        g_m = r2(TT * E0).rearrange("p (t e) -> p t e", e=E0)
        g_t = r2(TT * E0).rearrange("p (t e) -> p t e", e=E0)
        g_mb = r2(TT * E0 // 2, BF16).rearrange("p (t e) -> p t e", e=E0)
        g_w = r2(TT * E0).rearrange("p (t e) -> p t e", e=E0)
        g_s = r2(TT).rearrange("p (t e) -> p t e", e=1)
        used[0] = 0
        f_lg = r2(TT * 8).rearrange("p (t e) -> p t e", e=8)
        f_v8 = r2(TT * 8).rearrange("p (t e) -> p t e", e=8)
        f_i8 = r2(TT * 8, U32).rearrange("p (t e) -> p t e", e=8)
        f_if = r2(TT * 8).rearrange("p (t e) -> p t e", e=8)
        f_m = r2(TT * 8).rearrange("p (t e) -> p t e", e=8)
        f_mb = r2(TT * 8 // 2, BF16).rearrange("p (t e) -> p t e", e=8)
        f_n = r2(8)
        f_nb = r2(8)
        f_c = r2(8)
        f_t = r2(TT * 8).rearrange("p (t e) -> p t e", e=8)
        f_s = r2(TT)
        f_si = r2(TT, I32)
        f_be = r2(16)
        f_bi = r2(16, I32)
        f_cmp = r2(16 * 8).rearrange("p (j e) -> p j e", e=8)
        f_a = r2(8)
        xg = r2(NBLK * D).rearrange("p (j n) -> p j n", j=NBLK)
        xgT = [r2(C * P).rearrange("p (c n) -> p c n", c=C) for _ in range(2)]
        hT = [r2(DH).rearrange("p (k n) -> p k n", k=HC) for _ in range(2)]
        y_f = r2(NBLK * D).rearrange("p (j n) -> p j n", j=NBLK)
        y_back = r2(TT * D).rearrange("p (t n) -> p t n", t=TT)

        ps = ctx.enter_context(nc.psum_tensor("ps", [P, 8, 512], F32))

        def bank(i, n=512):
            return ps[:, i, 0:n]

        ident = cf[:, 0:128]
        vmask = cf[:, CF["vmask"]:CF["vmask"] + 4]
        iota = cf[:, CF["iota"]:CF["iota"] + 128]
        ident_b = cb[:, 0:128]
        mask_b = cb[:, CB["mask"]:CB["mask"] + 512]
        upper_b = cb[:, CB["upper"]:CB["upper"] + 128]
        ones_b = cb[:, CB["ones"]:CB["ones"] + 128]

        def w(key, at, n):
            o = W_COLS[key] + at
            return lambda c, lo=0, k=n: wall[:, c, o + lo:o + lo + k]

        def chunks_by(u):
            return min(32 * NB, 34 + 3 * (u + 1), 42 + -(-32 * (u + 1) // KT_N))

        def sems(prefix, names):
            return {n: sem(f"{prefix}_{n}") for n in names.split()}

        const_in = sem("const_in")
        wall_in = sem("wall_in")
        wall_late_in = sem("wall_late_in")
        wkv_in = sem("wkv_in")
        misc_in = sem("misc_in")
        ctx_in = [sem(f"ctx_in{i}") for i in range(3)]
        prep = sem("prep")
        var_ready = sem("var_ready")
        rstd_ready = sem("rstd_ready")
        dve_chain = [sem("dve_chain"), 0]
        pool_chain = [sem("pool_chain"), 0]

        kv = sems("kv", "proj turn_sb turned raw split dup keys_ps keys_lo keys_hi vals")
        ATT = "ln xt_ps xt bk q_ps k_ps v_ps lat_ps lat qe ke ve v0 xb sc z ex pt_ps pt pv y yt_ps yt o_ps x"
        PER_STAGE = {"ln": TT, "xt_ps": 2, "xt": 2, "bk": 1, "q_ps": 2, "k_ps": 2, "v_ps": NB, "lat_ps": 0, "lat": 0,
                     "qe": 2, "ke": 8, "ve": 4, "v0": 1, "xb": 1, "sc": TT, "z": TT, "ex": TT, "pt_ps": TT, "pt": 2 * TT,
                     "pv": TT, "y": TT, "yt_ps": 2, "yt": 2, "o_ps": TT, "x": TT}
        att = sems("attn", ATT)
        st = {n: {**att, "stage": i} for i, n in enumerate(("0x", "0a", "1a"))}

        st["0x"]["front"] = 6

        def base(s, name):
            return s["stage"] * PER_STAGE[name] if "stage" in s else 0

        mq = sems("mq", "ln xt_ps xt q_ps qf qs qdup qt_ps qt a_ps a_max nm row_ps row s_ps exp pv o o_ps y y_ps yt out_ps x")
        m0 = sems("m0", "ln xt_ps xt x_hi x_lo log_ps sig mask pos_ps gate gt_ps gt up_a up_b silu t g r hi mid lo down x gates_out")
        gb_in = [sem(f"gb_in{i}") for i in range(4)]
        w0_in = [sem(f"w0_in{i}") for i in range(4)]
        m1 = sems("m1", "zero zeroed ln xt_ps xt log_ps mask pos_ps slot sent h_ps act y_ps y back out xg_ps xgt")
        w1_in = [sem(f"w1_in{i}") for i in range(WSLOTS)]
        w2_in = [sem(f"w2_in{i}") for i in range(WSLOTS)]
        bias_in = sem("bias_in")
        more_bias_in = sem("more_bias_in")
        stored = sem("stored")
        XG = [(0, 1), (1, 5), (5, NBLK)]
        xg_in = [sem(f"xg_in{i}") for i in range(len(XG))]
        out_done = sem("out_done")

        def link(eng, chain, ins):
            chain[1] += 1
            ins.then_inc(chain[0], 1)
            eng.wait_ge(chain[0], chain[1])

        def bc(ap, shape):
            return ap.to_broadcast(shape)

        CFG = {"0x": (True, "0x_q", "0x_k", "0x_v", "0x_o", srcT),
               "0a": (False, "0a_q", "0a_k", "0a_v", "0a_o", xnT),
               "1a": (True, "1a_q", "1a_k", "1a_v", "1a_o", xnT)}

        block = ctx.enter_context(nc.Block())

        @block.sync
        def _(sp):
            sp.dma_start(wkv_sb[:], a["wkv"].rearrange("(c p) n -> p c n", p=P)).then_inc(wkv_in, 16)
            sp.dma_start(cf[:], a["cf"]).then_inc(const_in, 16)
            sp.dma_start(cb[:], a["cb"]).then_inc(const_in, 16)
            sp.wait_ge(prep, 3)
            for b in range(NB):
                if b >= 3:
                    sp.wait_ge(kv["proj"], b - 2)
                sp.dma_start(ctx_ring[b % 3][:, :, 0:S],
                             a["ctxT"][b].rearrange("(c p) s -> p c s", p=P)).then_inc(ctx_in[b % 3], 16)
            sp.dma_start(wall[:, :, 4 * D:W_TOTAL], a["wall"].rearrange("(c p) n -> p c n", p=P)[:, :, 4 * D:W_TOTAL]).then_inc(wall_late_in, 16)
            sp.wait_ge(m1["zero"], 1)
            sp.dma_start(scratch_x.rearrange("(j p) n -> p j n", p=P),
                         bc(zero_f[:].unsqueeze(1), [P, NBLK, D])).then_inc(m1["zeroed"], 16)
            sp.wait_ge(kv["proj"], NB)
            sp.wait_ge(m0["ln"], TT)
            for n in range(4):
                sp.dma_start(w0[n], a["moe0"][n]).then_inc(w0_in[n], 16)
            sp.wait_ge(m0["gt"], 1)
            sp.dma_start(scratch_g, gT[0:E0, :]).then_inc(m0["gates_out"], 16)
            sp.wait_ge(m0["gates_out"], 16)
            for n in range(1, E0T):
                if n >= 4:
                    sp.wait_ge(m0["down"], n - 3)
                    sp.dma_start(w0[n % 4], a["moe0"][n]).then_inc(w0_in[n % 4], 16)
                sp.dma_start(gb[n % 4], scratch_g[n - 1:n, :].partition_broadcast(P)).then_inc(gb_in[n % 4], 16)
            w1_v = a["w1"].rearrange("e (c p) n -> e p c n", p=P)
            w2_v = a["w2"].rearrange("e (k p) n -> e p k n", p=P)

            def expert(j):
                return j if j < E1 else sp.value_load(f_bi[0:1, j - E1:j - E1 + 1], min_val=0, max_val=E1 - 1)

            def load_w1(j):
                sp.dma_start(w1_s[j % WSLOTS], w1_v[bass.ds(expert(j), 1)].rearrange("e p c n -> p (e c) n")).then_inc(w1_in[j % WSLOTS], 16)

            def load_w2(j):
                sp.dma_start(w2_s[j % WSLOTS], w2_v[bass.ds(expert(j), 1)].rearrange("e p k n -> p (e k) n")).then_inc(w2_in[j % WSLOTS], 16)

            def store(lo_, hi_):
                sp.wait_ge(m1["y"], hi_)
                sp.dma_start(scratch_y[lo_ * P:hi_ * P, :].rearrange("(j p) n -> p j n", p=P), y_f[:, lo_:hi_, :]).then_inc(stored, 16)

            sp.wait_ge(m0["down"], E0T)
            load_w1(0)
            load_w2(0)
            load_w1(1)
            load_w2(1)
            load_w1(2)
            sp.wait_ge(mq["pv"], NB * KT_N)
            sp.dma_start(b1_s[:, 0:E1, :], a["b1"]).then_inc(bias_in, 16)
            sp.dma_start(b2_s[:, 0:E1, :].rearrange("p j n -> p (j n)"), a["b2row"].partition_broadcast(P)).then_inc(bias_in, 16)
            load_w2(2)
            load_w1(3)
            load_w2(3)
            sp.wait_ge(m1["slot"], 2)
            for j in range(E1, NBLK):
                e = expert(j)
                sp.dma_start(b1_s[:, j:j + 1, :], a["b1"][:, bass.ds(e, 1), :]).then_inc(more_bias_in, 16)
                sp.dma_start(b2_s[:, j, :], a["b2"][bass.ds(e, 1)].partition_broadcast(P)).then_inc(more_bias_in, 16)
            for j in range(WSLOTS, NBLK):
                sp.wait_ge(m1["h_ps"], 2 * (j - WSLOTS + 1))
                load_w1(j)
                sp.wait_ge(m1["y_ps"], j - WSLOTS + 1)
                load_w2(j)
                if j == 7:
                    store(0, 4)
            store(4, 8)
            store(8, 10)
            store(10, NBLK)
            sp.wait_ge(m1["out"], 1)
            sp.dma_start(out.rearrange("(t p) n -> p t n", p=P), x[:]).then_inc(out_done, 16)
            sp.wait_ge(out_done, 16)

        @block.gpsimd
        def _(pool):
            def lk(ins):
                link(pool, pool_chain, ins)

            for i in range(3):
                pool.memset(ctx_ring[i][:, :, S:SP], 0.0).then_inc(prep, 1)
            for i in range(2):
                pool.memset(Ks[i][:, :, KQ:KQ2], 1.0).then_inc(prep, 1)
            lk(pool.memset(v_ctx[:], 0.0))
            lk(pool.memset(v_ctx[:, :, :, 16:17], 1.0))
            pool.memset(zero_f[:], 0.0).then_inc(m1["zero"], 1)
            lk(pool.memset(v_sm, 0.0))
            pool.memset(v_sm[0:64, :, :, 32:33], 1.0).then_inc(st["0x"]["v0"], 1)
            pool.memset(v_sm[64:128, :, :, 33:34], 1.0).then_inc(st["0x"]["v0"], 1)
            pool.wait_ge(st["0x"]["v0"], 2)

            def context_tile(b):
                pool.wait_ge(kv["raw"], b + 1)
                pool.tensor_copy(v_ctx[:, b, :, 0:16], kvs[b % 2][:, :, 16:32]).then_inc(kv["vals"], 1)
                k6 = Ks[b % 2][:, :, 0:KQ].rearrange("p t (g d) -> p t g d", d=HD)
                pool.wait_ge(kv["split"], b + 1)
                pool.tensor_copy(k6[:, :, 2], k6[:, :, 0])
                pool.tensor_copy(k6[:, :, 4], k6[:, :, 0])
                pool.tensor_copy(k6[:, :, 5], k6[:, :, 1]).then_inc(kv["dup"], 3)

            roots = [0]

            def root():
                roots[0] += 1
                pool.wait_ge(var_ready, roots[0])
                lk(pool.tensor_scalar(rstd[:], mv[:, :, 1:2], EPS, None, ALU.add))
                pool.tensor_tensor(rstd[:], rstd[:], cf[:, CF["power"]:CF["power"] + TT].unsqueeze(2), ALU.pow).then_inc(rstd_ready, 1)

            def attn(n, clear):
                s = st[n]
                src_x = xn if n == "1a" else x
                o = BR[n + "_o"]
                if clear:
                    lk(pool.memset(v_sm, 0.0))
                    pool.memset(v_sm[0:64, :, :, 32:33], 1.0).then_inc(s["v0"], 1)
                    pool.memset(v_sm[64:128, :, :, 33:34], 1.0).then_inc(s["v0"], 1)
                    pool.wait_ge(s["v0"], 4)
                root()
                pool.wait_ge(s["ln"], base(s, "ln") + TT)
                pool.tensor_tensor(xb[:], src_x[:], bc(brow[:, o:o + D].unsqueeze(1), [P, TT, D]),
                                   ALU.add).then_inc(s["xb"], 1)
                if n == "1a":
                    root()

            context_tile(0)
            pool.wait_ge(misc_in, 16 * 6)
            pool.wait_ge(const_in, 32)
            attn("0x", False)
            for b in range(1, NB):
                context_tile(b)
            attn("0a", False)
            root()
            pool.wait_ge(m0["ln"], TT)
            for n in range(E0T):
                pool.wait_ge(m0["hi"], n + 1)
                if n >= 2:
                    pool.wait_ge(m0["lo"], n - 1)
                pool.tensor_tensor(hr[n % 2], t2[n % 2], hp[n % 4][0], ALU.subtract).then_inc(m0["r"], 1)
            root()
            for t in range(TT):
                Qg = Qs[:, t * H:(t + 1) * H, :].rearrange("p a (g d) -> p a g d", d=HD)
                pool.wait_ge(mq["qf"], t + 1)
                pool.tensor_copy(Qg[:, :, 1], Qg[:, :, 0])
                pool.tensor_copy(Qg[:, :, 3], Qg[:, :, 0])
                pool.wait_ge(mq["qs"], 2 * t + 1)
                pool.tensor_copy(Qg[:, :, 5], Qg[:, :, 2]).then_inc(mq["qdup"], 1)
            pool.wait_ge(mq["x"], TT)
            attn("1a", True)
            root()
            pool.wait_ge(m1["ln"], TT)
            pool.wait_ge(m1["zeroed"], 16)
            pool.wait_ge(m1["slot"], 2)
            for t in range(TT):
                pool.indirect_dma_start(
                    out=scratch_x[:, :], out_offset=bass.IndirectOffsetOnAxis(ap=f_si[:, t:t + 1], axis=0),
                    in_=xn[:, t, :], in_offset=None).then_inc(m1["sent"], 16)
            pool.wait_ge(stored, 16 * 4)
            for t in range(TT):
                pool.indirect_dma_start(
                    out=y_back[:, t, :], out_offset=None,
                    in_=scratch_y[:, :], in_offset=bass.IndirectOffsetOnAxis(ap=f_si[:, t:t + 1], axis=0)
                ).then_inc(m1["back"], 16)

        @block.scalar
        def _(act):
            wall_d = a["wall"].rearrange("(c p) n -> p c n", p=P)
            act.dma_start(x[:], a["x"].rearrange("(t p) n -> p t n", p=P)).then_inc(misc_in, 16)
            act.dma_start(srcT[:], a["ctx64T"].rearrange("(c p) n -> p c n", p=P)).then_inc(misc_in, 16)
            act.dma_start(bcol[:], a["bcol"]).then_inc(misc_in, 16)
            act.dma_start(brow[:], a["brow"].partition_broadcast(P)).then_inc(misc_in, 16)
            act.dma_start(wall[:, :, 0:4 * D], wall_d[:, :, 0:4 * D]).then_inc(wall_in, 16)
            act.dma_start(wkv_l[:], a["wkvl"]).then_inc(misc_in, 16)
            act.dma_start(gate_w[:], a["gate"].rearrange("(c p) n -> p c n", p=P)).then_inc(misc_in, 16)

            def kv_projected(b):
                act.wait_ge(kv["proj"], b + 1)
                if b >= 2:
                    act.wait_ge(kv["turned"], b - 1)
                act.activation(kvT_sb[b % 2][0:96, :], ps[0:96, b % 2, :], ACT.Copy)
                act.activation(kvT_sb[b % 2][96:128, 0:P], ps[96:128, b % 2, 0:P], ACT.Copy).then_inc(kv["turn_sb"], 2)

            def kv_turned(b):
                act.wait_ge(kv["turned"], b + 1)
                if b >= 2:
                    act.wait_ge(kv["vals"], b - 1)
                    act.wait_ge(kv["split"], b - 1)
                src = ps[:, 2 + b % 2, :].rearrange("p (u g n) -> p g u n", u=4, g=4)
                act.activation(kvs[b % 2][:, 0:12, :].rearrange("p (g u) n -> p g u n", g=3), src[:, 0:3], ACT.Copy)
                act.activation(kvs[b % 2][:, 12, :], src[:, 3, 0], ACT.Copy).then_inc(kv["raw"], 1)

            def keys_turned(b):
                act.wait_ge(kv["keys_ps"], b + 1)
                act.activation(kT[0:KQ2, b, 0:1024], ps[0:KQ2, 4, :].bitcast(BF16), ACT.Copy).then_inc(kv["keys_lo"], 1)

            def turned_x(s):
                act.wait_ge(s["xt_ps"], base(s, "xt_ps") + 1)
                act.activation(xnT[:, 0, :], bank(s.get("front", 0)), ACT.Copy).then_inc(s["xt"], 1)

            def attn_front(n):
                masked, qb, kb, vb, ob, src = CFG[n]
                s = st[n]
                f = s.get("front", 0)
                turned_x(s)
                yield
                if n == "0a":
                    act.wait_ge(s["lat_ps"], base(s, "lat_ps") + 1)
                    act.activation(lat[0:64, :], ps[0:64, 6, :], ACT.Identity, bias=bcol[0:64, BC_L:BC_L + 1]).then_inc(s["lat"], 1)
                for m in range(C):
                    act.wait_ge(s["q_ps"], base(s, "q_ps") + m + 1)
                    act.activation(q_T[:, m, :], bank((f or 2) + m), ACT.Identity,
                                   bias=bcol[:, BC[qb] + m:BC[qb] + m + 1]).then_inc(s["qe"], 1)
                yield
                act.wait_ge(s["k_ps"], base(s, "k_ps") + 2)
                act.wait_ge(s["bk"], base(s, "bk") + 1)
                for v in range(4):
                    act.activation(k_Tm[:, 1, v, :], bank((f or 4) + 1), ACT.Identity, bias=bkm[:, 1, v:v + 1],
                                   scale=vmask[:, v:v + 1]).then_inc(s["ke"], 1)
                yield
                act.wait_ge(s["v_ps"], base(s, "v_ps") + 4)
                if n != "0a":
                    act.wait_ge(s["v0"], 2 if s["stage"] == 0 else 4)
                for xh in range(2):
                    act.activation(v_sm[64 * xh:64 * xh + 64, 0:4, :, 16 * xh:16 * xh + 16],
                                   ps[64 * xh:64 * xh + 64, 6, :].rearrange("p (b j d) -> p b j d", b=4, j=8),
                                   ACT.Copy).then_inc(s["ve"], 1)
                yield

            def attn_back(n):
                masked, qb, kb, vb, ob, src = CFG[n]
                s = st[n]
                for i in range(TT + 1):
                    if i < TT:
                        act.wait_ge(s["z"], base(s, "z") + i + 1)
                        act.activation(z[i % 2], z[i % 2], ACT.Exp, scale=SCALE).then_inc(s["ex"], 1)
                    if i >= 1:
                        t = i - 1
                        act.wait_ge(s["pt_ps"], base(s, "pt_ps") + t + 1)
                        if t >= 2:
                            act.wait_ge(s["pv"], base(s, "pv") + t - 1)
                        act.activation(pT[t % 2][:, 0:4, :], bank(4).rearrange("p (j q) -> p j q", j=4), ACT.Copy).then_inc(s["pt"], 1)
                for c in range(C):
                    act.wait_ge(s["yt_ps"], base(s, "yt_ps") + c + 1)
                    act.activation(yT[:, c, :], bank(c), ACT.Identity,
                                   bias=bcol[:, BC[vb] + c:BC[vb] + c + 1]).then_inc(s["yt"], 1)

            def attn(n):
                for _ in attn_front(n):
                    pass
                attn_back(n)

            front = attn_front("0x")
            for i in range(NB + 2):
                if i < NB:
                    kv_projected(i)
                if 1 <= i <= NB:
                    kv_turned(i - 1)
                if i >= 2:
                    keys_turned(i - 2)
                if i == 1:
                    act.wait_ge(misc_in, 16 * 6)
                if 1 <= i <= 4:
                    next(front)
            attn_back("0x")
            attn("0a")
            turned_x(m0)
            act.wait_ge(m0["xt"], 2)
            act.activation(xp[0], xnT[:], ACT.Copy, scale=XS).then_inc(m0["x_hi"], 1)
            act.wait_ge(m0["log_ps"], 1)
            act.activation(g_sc, bank(4, TT * E0).rearrange("p (t e) -> p t e", e=E0), ACT.Exp, scale=-1.0 / XS).then_inc(m0["sig"], 1)

            def mid(n):
                act.wait_ge(m0["r"], n + 1)
                act.activation(hp[n % 4][1], hr[n % 2], ACT.Copy).then_inc(m0["mid"], 1)

            for n in range(E0T):
                act.wait_ge(m0["up_a"], n + 1)
                if n >= 2:
                    act.wait_ge(m0["t"], n - 1)
                act.activation(sa[n % 2], bank(n % 2), ACT.Silu, scale=1.0 / XS).then_inc(m0["silu"], 1)
                if n == 0:
                    act.wait_ge(m0["gt_ps"], 1)
                    act.activation(gT[0:E0, :], ps[0:E0, 5, :], ACT.Copy).then_inc(m0["gt"], 1)
                if n >= 1:
                    mid(n - 1)
                act.wait_ge(m0["g"], n + 1)
                if n >= 4:
                    act.wait_ge(m0["down"], n - 3)
                act.activation(hp[n % 4][0], t2[n % 2], ACT.Copy).then_inc(m0["hi"], 1)
            mid(E0T - 1)
            turned_x(mq)
            for t in range(TT):
                act.wait_ge(mq["q_ps"], t + 1)
                q_ps = bank(4 + t, D).rearrange("p (h d) -> p h d", h=H)
                act.mul(qf[:, t * H:(t + 1) * H, :], q_ps, SCALE)
                act.mul(Qs[:, t * H:(t + 1) * H, 0:HD], q_ps, SCALE).then_inc(mq["qf"], 1)
            for k in range(2 * TT):
                act.wait_ge(mq["qt_ps"], k + 1)
                t, h8 = k // 2, 8 * (k % 2)
                act.activation(QT[0:KQ, 2 * t:2 * t + 2, h8:h8 + 8, :].rearrange("p b h q -> p h b q"),
                               ps[0:KQ, k % 4, :].bitcast(BF16).rearrange("p (h b q) -> p h b q", h=8, b=2), ACT.Copy).then_inc(mq["qt"], 1)

            def rows(b):
                for r in range(2):
                    act.wait_ge(mq["row_ps"], 2 * b + r + 1)
                    t, b2 = b // 2, b % 2
                    act.activation(QT[KQ:KQ2, b, 8 * r:8 * r + 8, :],
                                   ps[KQ:KQ2, 6, :].rearrange("p (h q) -> p h q", h=8), ACT.Copy).then_inc(mq["row"], 1)

            rows(0)
            for b in range(NB):
                for k in range(KT_N):
                    u = b * KT_N + k
                    act.wait_ge(mq["s_ps"], u + 1)
                    if u >= NP_:
                        act.wait_ge(mq["pv"], u - NP_ + 1)
                    pr = 2 * (u % 2)
                    act.activation(probs[u % NP_], ps[:, pr:pr + 2, :].rearrange("p b n -> p (b n)"), ACT.Exp).then_inc(mq["exp"], 1)
                    if b >= 1 and k == 0:
                        act.wait_ge(mq["pv"], b * KT_N)
                        if b >= 3:
                            act.wait_ge(mq["o_ps"], b - 2)
                        act.activation(oT[(b - 1) % 2], bank(7, 256), ACT.Copy).then_inc(mq["o"], 1)
                    if b >= 1 and k == 5:
                        act.wait_ge(mq["y_ps"], b)
                        act.activation(yT[:, :, (b - 1) * T:b * T], ps[:, 6, 256:384].rearrange("p (x q) -> p x q", x=2), ACT.Copy).then_inc(mq["yt"], 1)
                    if b + 1 < NB and k == KT_N - 2:
                        rows(b + 1)
            act.wait_ge(mq["pv"], NB * KT_N)
            act.activation(oT[(NB - 1) % 2], bank(7, 256), ACT.Copy).then_inc(mq["o"], 1)
            act.wait_ge(mq["y_ps"], NB)
            act.activation(yT[:, :, (NB - 1) * T:NB * T], ps[:, 6, 256:384].rearrange("p (x q) -> p x q", x=2), ACT.Copy).then_inc(mq["yt"], 1)
            attn("1a")
            turned_x(m1)
            act.wait_ge(m1["zero"], 1)
            act.activation(gelu_warm[:], zero_f[:, 0:1], ACT.Gelu)

            act.wait_ge(m1["sent"], 16 * TT)
            for i, (lo_, hi_) in enumerate(XG):
                act.dma_start(xg[:, lo_:hi_, :], scratch_x[lo_ * P:hi_ * P, :].rearrange("(j p) n -> p j n", p=P)).then_inc(xg_in[i], 16)
            act.wait_ge(bias_in, 32)
            for j in range(NBLK):
                if j == E1:
                    act.wait_ge(more_bias_in, 32 * MORE)
                if j >= 2:
                    act.wait_ge(m1["y_ps"], j - 1)
                for hh in range(2):
                    act.wait_ge(m1["h_ps"], 2 * j + hh + 1)
                    for k in range(4 * hh, 4 * hh + 4):
                        ins = act.activation(hT[j % 2][:, k, :], ps[:, (1, 6)[j % 2] + hh, (k % 4) * P:(k % 4 + 1) * P],
                                             ACT.Gelu, bias=b1_s[:, j, k:k + 1])
                    ins.then_inc(m1["act"], 1)

        @block.vector
        def _(dve):
            def lk(ins):
                link(dve, dve_chain, ins)

            dve.wait_ge(prep, 5)
            def split_keys(b):
                kf = kvs[b % 2][:, :, 0:16]
                k6 = Ks[b % 2][:, :, 0:KQ].rearrange("p t (g d) -> p t g d", d=HD)
                dve.wait_ge(kv["raw"], b + 1)
                if b >= 2:
                    dve.wait_ge(kv["keys_ps"], b - 1)
                lk(dve.tensor_copy(k6[:, :, 0], kf))
                lk(dve.tensor_tensor(k_r1, kf, k6[:, :, 0], ALU.subtract))
                lk(dve.tensor_copy(k6[:, :, 1], k_r1))
                dve.tensor_tensor(k6[:, :, 3], k_r1, k6[:, :, 1], ALU.subtract).then_inc(kv["split"], 1)

            def keys_turned(b):
                dve.wait_ge(kv["keys_ps"], b + 1)
                dve.tensor_copy(kT[0:KQ2, b, 1024:SP], ps[0:KQ2, 5, :].bitcast(BF16)[:, 0:SP - 1024]).then_inc(kv["keys_hi"], 1)

            variances = [0]

            def normalise(src, dst, done):
                for t in range(TT):
                    ins = dve.bn_stats(stats[:, t, :], src[:, t, :])
                lk(ins)
                for t in range(TT):
                    ins = dve.bn_aggr(mv[:, t, :], stats[:, t, :])
                variances[0] += 1
                ins.then_inc(var_ready, 1)
                dve.wait_ge(rstd_ready, variances[0])
                for t in range(TT):
                    ins = dve.tensor_scalar(dst[:, t, :], src[:, t, :], mv[:, t, 0:1], rstd[:, t, :], ALU.subtract, ALU.mult)
                    if done is not None:
                        ins.then_inc(done, 1)
                if done is None:
                    lk(ins)

            def turned_x(s):
                dve.wait_ge(s["xt_ps"], base(s, "xt_ps") + 2)
                dve.tensor_copy(xnT[:, 1, :], bank(s.get("front", 0) + 1)).then_inc(s["xt"], 1)

            def attn_front(n):
                masked, qb, kb, vb, ob, src = CFG[n]
                s = st[n]
                f = s.get("front", 0)
                normalise(x, xn, s["ln"])
                for m in range(C):
                    ins = dve.tensor_scalar(bkm[:, m, :], vmask, bcol[:, BC[kb] + m:BC[kb] + m + 1], None, ALU.mult)
                ins.then_inc(s["bk"], 1)
                turned_x(s)
                yield
                dve.wait_ge(s["k_ps"], base(s, "k_ps") + 1)
                for v in range(4):
                    dve.tensor_scalar(k_Tm[:, 0, v, :], bank(f or 4), bcol[:, BC[kb]:BC[kb] + 1], vmask[:, v:v + 1],
                                      ALU.add, ALU.mult).then_inc(s["ke"], 1)
                yield
                dve.wait_ge(s["v_ps"], base(s, "v_ps") + 8)
                if n != "0a":
                    dve.wait_ge(s["v0"], 2 if s["stage"] == 0 else 4)
                for xh in range(2):
                    dve.tensor_copy(v_sm[64 * xh:64 * xh + 64, 4:8, :, 16 * xh:16 * xh + 16],
                                    ps[64 * xh:64 * xh + 64, 7, :].rearrange("p (b j d) -> p b j d", b=4, j=8)).then_inc(s["ve"], 1)
                yield

            def attn_back(n):
                masked, qb, kb, vb, ob, src = CFG[n]
                s = st[n]
                for i in range(TT + 2):
                    if i < TT:
                        b0 = 2 * (i % 2)
                        sc = ps[:, b0:b0 + 2, :].rearrange("p r (h k) -> p (r h) k", k=T)
                        dve.wait_ge(s["sc"], base(s, "sc") + i + 1)
                        lk(dve.tensor_reduce(mx[i % 2], sc, AX.X, ALU.max))
                        if i >= 2:
                            dve.wait_ge(s["pt_ps"], base(s, "pt_ps") + i - 1)
                        dve.tensor_tensor(z[i % 2].rearrange("p (h k) -> p h k", k=T), sc,
                                          bc(mx[i % 2].unsqueeze(2), [P, 16, T]), ALU.subtract).then_inc(s["z"], 1)
                    if 1 <= i <= TT:
                        t = i - 1
                        dve.wait_ge(s["pt_ps"], base(s, "pt_ps") + t + 1)
                        if t >= 2:
                            dve.wait_ge(s["pv"], base(s, "pv") + t - 1)
                        dve.tensor_copy(pT[t % 2][:, 4:8, :], bank(5).rearrange("p (j q) -> p j q", j=4)).then_inc(s["pt"], 1)
                    if i >= 2:
                        t = i - 2
                        o = bank(6 + t % 2, 272).rearrange("p (j n) -> p j n", n=34)
                        dve.wait_ge(s["pv"], base(s, "pv") + t + 1)
                        lk(dve.reciprocal(rs[t % 2], o[:, :, 32:34]))
                        dve.tensor_tensor(y_sm[:, t, :].rearrange("p (j x d) -> p j x d", j=8, x=2),
                                          o[:, :, 0:32].rearrange("p j (x d) -> p j x d", x=2),
                                          bc(rs[t % 2].unsqueeze(3), [P, 8, 2, HD]), ALU.mult).then_inc(s["y"], 1)
                dve.wait_ge(s["xb"], base(s, "xb") + 1)
                for t in range(TT):
                    dve.wait_ge(s["o_ps"], base(s, "o_ps") + t + 1)
                    at = bank(2 + t, D)
                    if n != "1a":
                        dve.tensor_tensor(x[:, t, :], at, xb[:, t, :], ALU.add).then_inc(s["x"], 1)
                    else:
                        ins = dve.tensor_tensor(un[:, t, :], at, xb[:, t, :], ALU.add)
                if n == "1a":
                    lk(ins)
                    normalise(un, un, None)
                    g_, b_ = BR["gamma"], BR["beta"]
                    lk(dve.tensor_tensor(un, un, bc(brow[:, g_:g_ + D].unsqueeze(1), [P, TT, D]), ALU.mult))
                    lk(dve.tensor_tensor(un, un, bc(brow[:, b_:b_ + D].unsqueeze(1), [P, TT, D]), ALU.add))
                    dve.tensor_tensor(x[:], x[:], un, ALU.add).then_inc(s["x"], TT)

            def after_stage(s):
                dve.wait_ge(s["x"], base(s, "x") + TT)

            def attn(n):
                for _ in attn_front(n):
                    pass
                attn_back(n)

            front = attn_front("0x")
            for i in range(NB + 1):
                if i < NB:
                    split_keys(i)
                if i >= 1:
                    keys_turned(i - 1)
                if i == 0:
                    dve.wait_ge(misc_in, 16 * 6)
                    dve.wait_ge(const_in, 32)
                if i in (0, 2, 3):
                    next(front)
            dve.wait_ge(kv["keys_lo"], NB)
            dve.wait_ge(kv["turned"], NB)
            dve.wait_ge(kv["dup"], 3 * NB)
            attn_back("0x")
            after_stage(st["0x"])
            attn("0a")
            after_stage(st["0a"])
            normalise(x, xn, m0["ln"])
            turned_x(m0)
            dve.wait_ge(m0["x_hi"], 1)
            dve.scalar_tensor_tensor(out=xp[1], in0=xnT[:], scalar=XS, in1=xp[0], op0=ALU.mult, op1=ALU.subtract).then_inc(m0["x_lo"], 1)
            dve.wait_ge(m0["sig"], 1)
            lk(dve.tensor_scalar(g_sc, g_sc, 1.0, None, ALU.add))
            lk(dve.reciprocal(g_sc, g_sc))
            lk(dve.tensor_tensor(g_sb, g_sc, bc(brow[:, BR_E:BR_E + E0].unsqueeze(1), [P, TT, E0]), ALU.add))
            for t in range(TT):
                ins = dve.max(g_v8[:, t, :], g_sb[:, t, :])
            lk(ins)
            for t in range(TT):
                ins = dve.max_index(g_i8[:, t, :], g_v8[:, t, :], g_sb[:, t, :])
            lk(ins)
            lk(dve.tensor_copy(g_f8, g_i8))
            io = bc(iota[:, 0:E0].unsqueeze(1), [P, TT, E0])
            lk(dve.tensor_tensor(g_m, io, bc(g_f8[:, :, 0:1], [P, TT, E0]), ALU.is_equal))
            for k in range(1, K0):
                lk(dve.tensor_tensor(g_t, io, bc(g_f8[:, :, k:k + 1], [P, TT, E0]), ALU.is_equal))
                lk(dve.tensor_tensor(g_m, g_m, g_t, ALU.add))
            dve.tensor_copy(g_mb, g_m).then_inc(m0["mask"], 1)
            lk(dve.tensor_tensor(g_w, g_sc, g_m, ALU.mult))
            lk(dve.tensor_reduce(g_s, g_w, AX.X, ALU.add))
            lk(dve.tensor_scalar(g_s, g_s, 1e-12, None, ALU.max))
            lk(dve.reciprocal(g_s, g_s))
            lk(dve.tensor_tensor(g_w, g_w, bc(g_s, [P, TT, E0]), ALU.mult))
            dve.wait_ge(m0["pos_ps"], 1)
            dve.scalar_tensor_tensor(out=g_w, in0=ps[:, 4, 128:256].rearrange("p (t e) -> p t e", e=E0),
                                     scalar=float(CAP), in1=g_w, op0=ALU.is_lt, op1=ALU.mult).then_inc(m0["gate"], 1)

            def lo(n):
                dve.wait_ge(m0["mid"], n + 1)
                dve.tensor_tensor(hp[n % 4][2], hr[n % 2], hp[n % 4][1], ALU.subtract).then_inc(m0["lo"], 1)

            for n in range(E0T):
                dve.wait_ge(m0["silu"], n + 1)
                dve.wait_ge(m0["up_b"], n + 1)
                if n >= 1:
                    dve.wait_ge(m0["g"], n)
                dst = tb if n else t2[0]
                ins = dve.scalar_tensor_tensor(out=dst, in0=bank(2 + n % 2), scalar=1.0 / XS, in1=sa[n % 2],
                                               op0=ALU.mult, op1=ALU.mult)
                ins.then_inc(m0["t"], 1)
                dve.wait_ge(m0["t"], n + 1)
                if n == 0:
                    dve.nop().then_inc(m0["g"], 1)
                else:
                    if n >= 2:
                        dve.wait_ge(m0["r"], n - 1)
                    dve.wait_ge(gb_in[n % 4], 16 * (n // 4 + (n % 4 != 0)))
                    dve.tensor_tensor(t2[n % 2], gb[n % 4], tb, ALU.mult).then_inc(m0["g"], 1)
                if n >= 1:
                    lo(n - 1)
            lo(E0T - 1)
            dve.wait_ge(m0["down"], E0T)
            dve.tensor_tensor(x[:], ps[:, 6:8, :].rearrange("p b (t n) -> p (b t) n", n=D), x[:], ALU.add).then_inc(m0["x"], TT)
            after_stage(m0)
            normalise(x, xn, mq["ln"])
            turned_x(mq)
            for t in range(TT):
                a_ = slice(t * H, (t + 1) * H)
                Qg = Qs[:, a_, :].rearrange("p a (g d) -> p a g d", d=HD)
                dve.wait_ge(mq["qf"], t + 1)
                lk(dve.tensor_tensor(q_r1[:, a_, :], qf[:, a_, :], Qg[:, :, 0], ALU.subtract))
                dve.tensor_copy(Qg[:, :, 2], q_r1[:, a_, :]).then_inc(mq["qs"], 1)
                dve.wait_ge(mq["qs"], 2 * t + 1)
                dve.tensor_tensor(Qg[:, :, 4], q_r1[:, a_, :], Qg[:, :, 2], ALU.subtract).then_inc(mq["qs"], 1)

            def maxima(lo_, hi_):
                for n in range(lo_, hi_):
                    b, q, c = n // 32, n % 32 // 4, n % 4
                    dve.wait_ge(mq["a_ps"], n + 1)
                    dve.tensor_reduce(mp[b % 2][:, q, c:c + 1], bank(4 + n % 2, CHUNKS[c][1]), AX.X, ALU.max).then_inc(mq["a_max"], 1)
                    if n % 32 == 31:
                        dve.wait_ge(mq["a_max"], 32 * (b + 1))
                        lk(dve.tensor_reduce(nm, mp[b % 2], AX.X, ALU.max, negate=True))
                        if b >= 2:
                            dve.wait_ge(mq["row_ps"], 2 * b - 2)
                        lk(dve.tensor_copy(NM[b % 2][:, :, 0], nm))
                        dve.tensor_tensor(NM[b % 2][:, :, 1], nm, NM[b % 2][:, :, 0], ALU.subtract).then_inc(mq["nm"], 1)

            def outputs(b):
                dve.wait_ge(mq["o_ps"], b + 1)
                o = ps[:, 6, 0:256].rearrange("p (t c n) -> p t c n", t=2, c=4)
                lk(dve.reciprocal(rc[b % 2], o[:, :, :, 16]))
                if b >= 2:
                    dve.wait_ge(mq["y_ps"], b - 1)
                dve.tensor_tensor(yn[b % 2].rearrange("p c t d -> p t c d"), o[:, :, :, 0:16],
                                  bc(rc[b % 2].unsqueeze(3), [P, 2, 4, HD]), ALU.mult).then_inc(mq["y"], 1)

            maxima(0, chunks_by(-1))
            for u in range(NB * KT_N):
                maxima(chunks_by(u - 1), chunks_by(u))
                if u >= KT_N and u % KT_N == 3:
                    outputs(u // KT_N - 1)
            outputs(NB - 1)
            for t in range(TT):
                dve.wait_ge(mq["out_ps"], t + 1)
                dve.tensor_tensor(x[:, t, :], bank(t, D), x[:, t, :], ALU.add).then_inc(mq["x"], 1)
            after_stage(mq)
            attn("1a")
            after_stage(st["1a"])
            normalise(x, xn, m1["ln"])
            turned_x(m1)
            dve.wait_ge(m1["log_ps"], 1)
            lk(dve.tensor_tensor(f_lg, bank(2, TT * 8).rearrange("p (t e) -> p t e", e=8),
                                 bc(brow[:, BR_G:BR_G + 8].unsqueeze(1), [P, TT, 8]), ALU.add))
            for t in range(TT):
                ins = dve.max(f_v8[:, t, :], f_lg[:, t, :])
            lk(ins)
            for t in range(TT):
                ins = dve.max_index(f_i8[:, t, :], f_v8[:, t, :], f_lg[:, t, :])
            lk(ins)
            lk(dve.tensor_copy(f_if, f_i8))
            lk(dve.tensor_tensor(f_m, bc(iota[:, 0:8].unsqueeze(1), [P, TT, 8]), bc(f_if[:, :, 0:1], [P, TT, 8]), ALU.is_equal))
            dve.tensor_copy(f_mb, f_m).then_inc(m1["mask"], 1)
            dve.wait_ge(m1["pos_ps"], 1)
            lk(dve.tensor_copy(f_n, ps[:, 2, 128:136]))
            lk(dve.tensor_scalar(f_nb, f_n, float(P), None, ALU.is_gt))
            for k in range(2, TT):
                lk(dve.scalar_tensor_tensor(out=f_nb, in0=f_n, scalar=float(k * P), in1=f_nb, op0=ALU.is_gt, op1=ALU.add))
            lk(dve.tensor_copy(f_c, f_nb))
            for e in range(1, E1):
                lk(dve.tensor_tensor(f_c[:, e:e + 1], f_c[:, e:e + 1], f_c[:, e - 1:e], ALU.add))
            lk(dve.tensor_tensor(f_cmp, bc(f_c.unsqueeze(1), [P, 16, 8]), bc(cf[:, CF["blk"]:CF["blk"] + 16].unsqueeze(2), [P, 16, 8]), ALU.is_le))
            lk(dve.tensor_reduce(f_be, f_cmp, AX.X, ALU.add))
            lk(dve.tensor_scalar(f_be, f_be, float(E1 - 1), None, ALU.min))
            dve.tensor_copy(f_bi, f_be).then_inc(m1["slot"], 1)
            lk(dve.tensor_tensor(f_c, f_c, f_nb, ALU.subtract))
            lk(dve.scalar_tensor_tensor(out=f_a, in0=f_c, scalar=float(E1 - 1), in1=iota[:, 0:8], op0=ALU.add, op1=ALU.subtract))
            pos = ps[:, 2, 64:96].rearrange("p (t e) -> p t e", e=8)
            lk(dve.scalar_tensor_tensor(out=f_t, in0=pos, scalar=float(P), in1=bc(f_a.unsqueeze(1), [P, TT, 8]), op0=ALU.is_ge, op1=ALU.mult))
            lk(dve.tensor_tensor(f_t, f_t, bc(iota[:, 0:8].unsqueeze(1), [P, TT, 8]), ALU.add))
            lk(dve.scalar_tensor_tensor(out=f_t, in0=f_t, scalar=float(P), in1=pos, op0=ALU.mult, op1=ALU.add))
            lk(dve.tensor_tensor(f_t, f_t, f_m, ALU.mult))
            lk(dve.tensor_reduce(f_s, f_t, AX.X, ALU.add))
            dve.tensor_copy(f_si, f_s).then_inc(m1["slot"], 1)

            def block_turned(j):
                dve.wait_ge(m1["xg_ps"], j + 1)
                if j >= 2:
                    dve.wait_ge(m1["h_ps"], 2 * (j - 1))
                dve.tensor_copy(xgT[j % 2], bank(0, D).rearrange("p (c n) -> p c n", c=C)).then_inc(m1["xgt"], 1)

            block_turned(0)
            block_turned(1)
            dve.wait_ge(bias_in, 32)
            for j in range(NBLK):
                if j + 2 < NBLK:
                    block_turned(j + 2)
                if j == E1:
                    dve.wait_ge(more_bias_in, 32 * MORE)
                dve.wait_ge(m1["y_ps"], j + 1)
                dve.tensor_tensor(y_f[:, j, :], bank(3 + j % 2, D), b2_s[:, j, :], ALU.add).then_inc(m1["y"], 1)
            dve.wait_ge(m1["back"], 16 * TT)
            dve.tensor_tensor(x[:], x[:], y_back, ALU.add).then_inc(m1["out"], 1)

        @block.tensor
        def _(pe):
            pe.wait_ge(const_in, 32)
            pe.wait_ge(wkv_in, 16)
            pe.wait_ge(prep, 3)
            def kv_project(b):
                pe.wait_ge(ctx_in[b % 3], 16 * (b // 3 + 1))
                if b >= 2:
                    pe.wait_ge(kv["turn_sb"], 2 * (b - 1))
                for c in range(C):
                    for g in range(4):
                        n = 512 if g < 3 else P
                        ins = pe.matmul(ps[32 * g:32 * g + 32, b % 2, 0:n], wkv_sb[:, c, :], ctx_ring[b % 3][:, c, 512 * g:512 * g + n],
                                        start=(c == 0), stop=(c == C - 1))
                ins.then_inc(kv["proj"], 1)

            def kv_turn(b):
                pe.wait_ge(kv["turn_sb"], 2 * (b + 1))
                if b >= 2:
                    pe.wait_ge(kv["raw"], b - 1)
                for u in range(4):
                    r = P if u == 0 else 96
                    ins = pe.transpose(ps[:, 2 + b % 2, u * P:u * P + r], kvT_sb[b % 2][0:r, u * P:(u + 1) * P], ident[0:r, 0:r])
                ins.then_inc(kv["turned"], 1)

            def keys_turn(b):
                pe.wait_ge(kv["dup"], 3 * (b + 1))
                pe.wait_ge(kv["split"], b + 1)
                if b >= 1:
                    pe.wait_ge(kv["keys_lo"], b)
                    pe.wait_ge(kv["keys_hi"], b)
                for t in range(KT_N):
                    at = ps[0:KQ2, 4 + t // 8, :].bitcast(BF16)[:, (t % 8) * P:(t % 8 + 1) * P]
                    ins = pe.transpose(at, Ks[b % 2][:, t, 0:KQ2], ident_b)
                ins.then_inc(kv["keys_ps"], 1)

            def turn_x(s):
                pe.wait_ge(s["ln"], base(s, "ln") + TT)
                for c in range(C):
                    for t in range(TT):
                        ins = pe.transpose(ps[:, s.get("front", 0) + c, t * P:(t + 1) * P], xn[:, t, c * P:(c + 1) * P], ident)
                    ins.then_inc(s["xt_ps"], 1)

            def mm2(dst, lhs, rhs):
                for c in range(C):
                    ins = pe.matmul(dst, lhs(c), rhs(c), start=(c == 0), stop=(c == C - 1))
                return ins

            def attn_front(n):
                masked, qb, kb, vb, ob, src = CFG[n]
                s = st[n]
                f = s.get("front", 0)
                if n == "0a":
                    wq, wl = w(n, 0, D), w(n, D, 64)
                else:
                    wq, wk, wv = (w(n, i * D, D) for i in range(3))
                turn_x(s)
                yield
                pe.wait_ge(s["xt"], base(s, "xt") + 2)
                if n == "0a":
                    mm2(ps[0:64, 6, :], lambda c: wl(c), lambda c: xnT[:, c, :]).then_inc(s["lat_ps"], 1)
                for m in range(C):
                    mm2(bank((f or 2) + m), lambda c: wq(c, m * P, P), lambda c: xnT[:, c, :]).then_inc(s["q_ps"], 1)
                yield
                if n == "0a":
                    pe.wait_ge(s["lat"], base(s, "lat") + 1)
                for m in range(C):
                    if f:
                        pe.wait_ge(s["qe"], m + 1)
                    if n == "0a":
                        ins = pe.matmul(bank(4 + m), wkv_l[:, m * P:(m + 1) * P], lat[0:64, :], start=True, stop=True)
                    else:
                        ins = mm2(bank((f or 4) + m), lambda c: wk(c, m * P, P), lambda c: src[:, c, :])
                    ins.then_inc(s["k_ps"], 1)
                yield
                if f:
                    pe.wait_ge(s["ke"], 8)
                for b in range(NB):
                    for c in range(1 if n == "0a" else C):
                        for xh in range(2):
                            dst = ps[64 * xh:64 * xh + 64, 6 + b // 4, (b % 4) * P:(b % 4 + 1) * P]
                            if n == "0a":
                                lhs, rhs = lat[0:64, b * T:(b + 1) * T], wkv_l[:, D:2 * D]
                            else:
                                lhs, rhs = src[:, c, b * T:(b + 1) * T], wv(c)
                            ins = pe.matmul(dst, lhs, rhs.rearrange("p (j x d) -> p j x d", j=8, x=2)[:, :, xh],
                                            start=(c == 0), stop=(n == "0a" or c == C - 1))
                    ins.then_inc(s["v_ps"], 1)
                pe.wait_ge(s["qe"], base(s, "qe") + 2)
                pe.wait_ge(s["ke"], base(s, "ke") + 8)
                yield

            def attn_back(n):
                masked, qb, kb, vb, ob, src = CFG[n]
                s = st[n]
                wo = w(n, D + 64 if n == "0a" else 3 * D, D)

                def scores(t):
                    b0 = 2 * (t % 2)
                    if t >= 2:
                        pe.wait_ge(s["z"], base(s, "z") + t - 1)
                    if masked:
                        for r in range(2):
                            pe.matmul(bank(b0 + r), ident_b, mask_b, start=True, stop=False, skip_group_check=True)
                    for m in range(C):
                        for r in range(2):
                            for b2 in range(2):
                                q0 = (2 * t + b2) * T
                                rr = slice(64 * r, 64 * r + 64)
                                ins = pe.matmul(ps[64 * b2:64 * b2 + 64, b0 + r, m * 256:(m + 1) * 256],
                                                q_T[rr, m, q0:q0 + T], k_Tm[rr, m, :, q0:q0 + T],
                                                start=not masked, stop=True, skip_group_check=True)
                    ins.then_inc(s["sc"], 1)

                def turn_probs(t):
                    pe.wait_ge(s["ex"], base(s, "ex") + t + 1)
                    if t >= 1:
                        pe.wait_ge(s["pt"], base(s, "pt") + 2 * t)
                    zv = z[t % 2].rearrange("p (r m v k) -> p r m (v k)", r=2, m=2, v=4)
                    for j in range(8):
                        m, r, vp = j // 4, (j // 2) % 2, j % 2
                        ins = pe.transpose(ps[:, 4 + j // 4, (j % 4) * P:(j % 4 + 1) * P],
                                           zv[:, r, m, vp * P:(vp + 1) * P], ident)
                    ins.then_inc(s["pt_ps"], 1)

                def values(t):
                    pe.wait_ge(s["pt"], base(s, "pt") + 2 * t + 2)
                    if t >= 2:
                        pe.wait_ge(s["y"], base(s, "y") + t - 1)
                    for j in range(8):
                        for b2 in range(2):
                            ins = pe.matmul(ps[64 * b2:64 * b2 + 64, 6 + t % 2, j * 34:(j + 1) * 34],
                                            pT[t % 2][:, j, 64 * b2:64 * b2 + 64], v_sm[:, 2 * t + b2, j, :],
                                            start=True, stop=True, skip_group_check=True)
                    ins.then_inc(s["pv"], 1)

                for i in range(TT + 2):
                    if i < TT:
                        scores(i)
                    if 1 <= i <= TT:
                        turn_probs(i - 1)
                    if i >= 2:
                        if i == 2:
                            pe.wait_ge(s["ve"], base(s, "ve") + 4)
                        values(i - 2)
                pe.wait_ge(s["y"], base(s, "y") + TT)
                for c in range(C):
                    for t in range(TT):
                        ins = pe.transpose(ps[:, c, t * P:(t + 1) * P], y_sm[:, t, c * P:(c + 1) * P], ident)
                    ins.then_inc(s["yt_ps"], 1)
                pe.wait_ge(s["yt"], base(s, "yt") + 2)
                for t in range(TT):
                    mm2(bank(2 + t, D), lambda c: yT[:, c, t * P:(t + 1) * P],
                        lambda c: wo(c)).then_inc(s["o_ps"], 1)

            def attn(n):
                for _ in attn_front(n):
                    pass
                attn_back(n)

            front = attn_front("0x")
            for i in range(NB + 2):
                if i < NB:
                    kv_project(i)
                if 1 <= i <= NB:
                    kv_turn(i - 1)
                if i == 2:
                    pe.wait_ge(prep, 5)
                if i >= 2:
                    keys_turn(i - 2)
                if i == 1:
                    pe.wait_ge(wall_in, 16)
                    pe.wait_ge(misc_in, 16 * 6)
                if 1 <= i <= 4:
                    next(front)
            pe.wait_ge(kv["raw"], NB)
            pe.wait_ge(kv["keys_lo"], NB)
            pe.wait_ge(kv["keys_hi"], NB)
            attn_back("0x")
            pe.wait_ge(wall_late_in, 16)
            attn("0a")
            turn_x(m0)
            pe.wait_ge(m0["x_lo"], 1)
            for t in range(TT):
                for k in range(2):
                    for c in range(C):
                        ins = pe.matmul(ps[:, 4, t * E0:(t + 1) * E0], xp[k][:, c, t * P:(t + 1) * P], gate_w[:, c, :],
                                        start=(k == 0 and c == 0), stop=(k == 1 and c == 1), skip_group_check=True)
            ins.then_inc(m0["log_ps"], 1)
            def up(n):
                wn = w0[n % 4]
                pe.wait_ge(w0_in[n % 4], 16 * (n // 4 + 1))
                if n >= 2:
                    pe.wait_ge(m0["t"], n - 1)
                for half, dst in ((0, n % 2), (1, 2 + n % 2)):
                    for c in range(C):
                        for k in range(2):
                            ins = pe.matmul(bank(dst), wn[:, c * 256 + half * 128:c * 256 + half * 128 + 128], xp[k][:, c, :],
                                            start=(c == 0 and k == 0), stop=(c == 1 and k == 1))
                    ins.then_inc(m0["up_a" if half == 0 else "up_b"], 1)

            up(0)
            up(1)
            pe.wait_ge(m0["mask"], 1)
            for t in range(TT):
                for k in range(t + 1):
                    ins = pe.matmul(ps[:, 4, 128 + t * E0:128 + (t + 1) * E0], upper_b if k == t else ones_b, g_mb[:, k, :],
                                    start=(k == 0), stop=(k == t), skip_group_check=True)
            ins.then_inc(m0["pos_ps"], 1)
            pe.wait_ge(m0["gate"], 1)
            for t in range(TT):
                ins = pe.transpose(ps[0:E0, 5, t * P:(t + 1) * P], g_w[:, t, :], ident)
            ins.then_inc(m0["gt_ps"], 1)

            def down(n):
                pe.wait_ge(m0["lo"], n + 1)
                for t in range(TT):
                    for k in range(3):
                        ins = pe.matmul(ps[:, 6 + t // 2, (t % 2) * D:(t % 2) * D + D], hp[n % 4][k][:, t * P:(t + 1) * P],
                                        w0[n % 4][:, 512:768], start=(n == 0 and k == 0 and t % 2 == 0),
                                        stop=(n == E0T - 1 and k == 2), skip_group_check=True)
                ins.then_inc(m0["down"], 1)

            for n in range(E0T):
                if n >= 2:
                    up(n)
                if n >= 2:
                    down(n - 2)
            down(E0T - 2)
            down(E0T - 1)
            wq, wo = w("1x", 0, D), w("1x", D + 32, D)
            turn_x(mq)
            pe.wait_ge(mq["xt"], 2)
            for t in range(TT):
                mm2(bank(4 + t, D), lambda c: xnT[:, c, t * P:(t + 1) * P], lambda c: wq(c)).then_inc(mq["q_ps"], 1)

            def turn_queries(t):
                pe.wait_ge(mq["qs"], 2 * t + 2)
                pe.wait_ge(mq["qdup"], t + 1)
                if t >= 2:
                    pe.wait_ge(mq["qt"], 2 * (t - 1))
                for k in range(2):
                    for i in range(8):
                        ins = pe.transpose(ps[0:KQ, 2 * (t % 2) + k, :].bitcast(BF16)[:, i * P:(i + 1) * P],
                                           Qs[:, t * H + 8 * k + i, :], ident_b)
                    ins.then_inc(mq["qt_ps"], 1)

            def maxima(lo_, hi_):
                for n in range(lo_, hi_):
                    b, q, c = n // 32, n % 32 // 4, n % 4
                    if n % 64 == 0:
                        pe.wait_ge(mq["qt"], 2 * (b // 2) + 2)
                    if n >= 2:
                        pe.wait_ge(mq["a_max"], n - 1)
                    pe.matmul(bank(4 + n % 2, CHUNKS[c][1]), QT[0:KQ, b, 2 * q:2 * q + 2, :].rearrange("p h q -> p (h q)"),
                              kT[0:KQ, b, CHUNKS[c][0]:CHUNKS[c][0] + CHUNKS[c][1]], start=True, stop=True).then_inc(mq["a_ps"], 1)

            def rows(b):
                pe.wait_ge(mq["nm"], b + 1)
                for r in range(2):
                    if 2 * b + r >= 1:
                        pe.wait_ge(mq["row"], 2 * b + r)
                    if r == 0 and b >= 2:
                        pe.wait_ge(mq["yt"], b - 1)
                    for q in range(4):
                        ins = pe.matmul(ps[KQ:KQ2, 6, q * P:(q + 1) * P], NM[b % 2][:, 4 * r + q, :], ident_b, start=True, stop=True, skip_group_check=True)
                    ins.then_inc(mq["row_ps"], 1)

            def scores(u):
                b, k = u // KT_N, u % KT_N
                t, b2 = b // 2, b % 2
                if k == 0:
                    pe.wait_ge(mq["row"], 2 * b + 2)
                if u >= 2:
                    pe.wait_ge(mq["exp"], u - 1)
                for h in range(2):
                    ins = pe.matmul(bank(2 * (u % 2) + h), kT[0:KQ2, b, k * P:(k + 1) * P],
                                    QT[0:KQ2, b, 8 * h:8 * h + 8, :].rearrange("p h q -> p (h q)"), start=True, stop=True)
                ins.then_inc(mq["s_ps"], 1)

            def values(u):
                b, k = u // KT_N, u % KT_N
                rows_ = P if k < KT_N - 1 else K_LAST
                pe.wait_ge(mq["exp"], u + 1)
                if k == 0 and b >= 1:
                    pe.wait_ge(mq["o"], b)
                for c in range(4):
                    ins = pe.matmul(ps[32 * c:32 * c + 32, 7, 0:256], v_ctx[0:rows_, b, k, :],
                                    probs[u % NP_][0:rows_, 256 * c:256 * c + 256], start=(k == 0), stop=(k == KT_N - 1),
                                    skip_group_check=True)
                ins.then_inc(mq["pv"], 1)

            def turn_out(b):
                pe.wait_ge(mq["o"], b + 1)
                pe.wait_ge(mq["row"], 2 * min(b + 2, NB))
                for t in range(2):
                    ins = pe.transpose(ps[:, 6, t * P:(t + 1) * P], oT[b % 2][:, t * P:(t + 1) * P], ident)
                ins.then_inc(mq["o_ps"], 1)

            def turn_y(b):
                pe.wait_ge(mq["y"], b + 1)
                pe.transpose(ps[:, 6, 256:384], yn[b % 2].rearrange("p c t d -> p (c t d)"), ident).then_inc(mq["y_ps"], 1)

            turn_queries(0)
            pe.wait_ge(mq["qf"], TT)
            maxima(0, 8)
            turn_queries(1)
            maxima(8, 14)
            turn_queries(2)
            maxima(14, 20)
            turn_queries(3)
            maxima(20, chunks_by(-1))
            rows(0)
            pe.wait_ge(mq["qt"], 2 * TT)
            scores(0)
            for u in range(NB * KT_N):
                b, k = u // KT_N, u % KT_N
                lo_, hi_ = chunks_by(u - 1), chunks_by(u)
                if k == KT_N - 2 and b + 1 < NB:
                    rows(b + 1)
                if u + 1 < NB * KT_N:
                    scores(u + 1)
                maxima(lo_, min(hi_, lo_ + 1))
                if u >= 1:
                    values(u - 1)
                maxima(min(hi_, lo_ + 1), hi_)
                if b >= 1 and k == 2:
                    turn_out(b - 1)
                if b >= 1 and k == 4:
                    turn_y(b - 1)
            values(NB * KT_N - 1)
            turn_out(NB - 1)
            turn_y(NB - 1)
            pe.wait_ge(mq["yt"], NB)
            for t in range(TT):
                mm2(bank(t, D), lambda c: yT[:, c, t * P:(t + 1) * P], lambda c: wo(c)).then_inc(mq["out_ps"], 1)
            attn("1a")
            wg = w("g", 0, E1)
            turn_x(m1)
            pe.wait_ge(m1["xt"], 2)
            for t in range(TT):
                ins = mm2(ps[:, 2, t * 8:(t + 1) * 8], lambda c: xnT[:, c, t * P:(t + 1) * P], lambda c: wg(c))
            ins.then_inc(m1["log_ps"], 1)
            pe.wait_ge(m1["mask"], 1)
            for t in range(TT):
                for k in range(t + 1):
                    pe.matmul(ps[:, 2, 64 + t * 8:64 + (t + 1) * 8], upper_b if k == t else ones_b, f_mb[:, k, :],
                              start=(k == 0), stop=(k == t), skip_group_check=True)
            for k in range(TT):
                ins = pe.matmul(ps[:, 2, 128:136], ones_b, f_mb[:, k, :], start=(k == 0), stop=(k == TT - 1), skip_group_check=True)
            ins.then_inc(m1["pos_ps"], 1)
            pe.wait_ge(m1["slot"], 2)

            def turn_block(j):
                for i, (lo_, _) in enumerate(XG):
                    if j == lo_:
                        pe.wait_ge(xg_in[i], 16)
                if j >= 1:
                    pe.wait_ge(m1["xgt"], j)
                for c in range(C):
                    ins = pe.transpose(ps[:, 0, c * P:(c + 1) * P], xg[:, j, c * P:(c + 1) * P], ident)
                ins.then_inc(m1["xg_ps"], 1)

            def up(j):
                pe.wait_ge(m1["xgt"], j + 1)
                pe.wait_ge(w1_in[j % WSLOTS], 16 * (j // WSLOTS + 1))
                for hh in range(2):
                    if j >= 2:
                        pe.wait_ge(m1["act"], 2 * (j - 2) + hh + 1)
                    for k in range(4 * hh, 4 * hh + 4):
                        ins = mm2(ps[:, (1, 6)[j % 2] + hh, (k % 4) * P:(k % 4 + 1) * P],
                                  lambda c: w1_s[j % WSLOTS][:, c, k * P:(k + 1) * P], lambda c: xgT[j % 2][:, c, :])
                    ins.then_inc(m1["h_ps"], 1)

            def down(j):
                pe.wait_ge(w2_in[j % WSLOTS], 16 * (j // WSLOTS + 1))
                if j >= 2:
                    pe.wait_ge(m1["y"], j - 1)
                for k in range(HC):
                    if k % 4 == 0:
                        pe.wait_ge(m1["act"], 2 * j + k // 4 + 1)
                    ins = pe.matmul(bank(3 + j % 2, D), hT[j % 2][:, k, :], w2_s[j % WSLOTS][:, k, :],
                                    start=(k == 0), stop=(k == HC - 1))
                ins.then_inc(m1["y_ps"], 1)

            turn_block(0)
            up(0)
            turn_block(1)
            for j in range(NBLK):
                if j + 1 < NBLK:
                    up(j + 1)
                if j + 2 < NBLK:
                    turn_block(j + 2)
                down(j)


def kernel(**inputs):
    import numpy as _np
    import concourse.bacc as _bacc
    from concourse.bass_utils import run_bass_kernel_spmd as _run

    g = {k: _np.asarray(v) for k, v in inputs.items()}
    cc = _np.ascontiguousarray

    def cols(b):
        return b.reshape(C, P).T

    ar = {}
    ar["x"] = cc(g["x"].reshape(TOK, D))
    ctx_ = g["ctx_1024"]
    ar["ctxT"] = cc(ctx_.transpose(0, 2, 1))
    ar["ctx64T"] = cc(ctx_[:, :T].reshape(TOK, D).T)
    wo1 = g["L1_xattn_Wo"].reshape(8, 2, HD, D).transpose(1, 0, 2, 3).reshape(D, D)
    ar["wall"] = cc(_np.concatenate([
        g["L0_xattn_Wq"].T, g["L0_xattn_Wk"].T, g["L0_xattn_Wv"].T, g["L0_xattn_Wo"].T,
        g["L0_attn_Wq"], g["L0_attn_Wl"], g["L0_attn_Wo"],
        g["L1_xattn_Wq"], g["L1_xattn_Wkv"], wo1,
        g["L1_attn_Wqkv"].T, g["L1_attn_Wout"].T, g["L1_ffn_Wg"]], axis=1))
    ar["wkv"] = cc(g["L1_xattn_Wkv"])
    ar["wkvl"] = cc(_np.concatenate([g["L0_attn_Wk"], g["L0_attn_Wv"]], axis=1))
    bq, bk, bv = g["L1_attn_bqkv"].reshape(3, D)
    bl = _np.zeros((P, 2), _np.float32)
    bl[:64, 0] = g["L0_attn_bl"]
    ar["bcol"] = cc(_np.concatenate([cols(v) for v in (
        g["L0_xattn_bq"], g["L0_xattn_bk"], g["L0_xattn_bv"],
        g["L0_attn_bq"], g["L0_attn_bk"], g["L0_attn_bv"], bq, bk, bv)] + [bl], axis=1))
    ar["brow"] = cc(_np.concatenate([g[k] for k in (
        "L0_xattn_bo", "L0_attn_bo", "L1_attn_bout", "L1_attn_gamma", "L1_attn_beta", "L0_ffn_bias", "L1_ffn_bg")])[None])
    ar["gate"] = cc(g["L0_ffn_gate_w"].T)
    bf = ar["gate"].dtype
    w1 = _np.concatenate([g["L0_ffn_sw1"].T[None], g["L0_ffn_W1"]])
    w3 = _np.concatenate([g["L0_ffn_sw3"].T[None], g["L0_ffn_W3"]])
    w2 = _np.concatenate([g["L0_ffn_sw2"].T[None], g["L0_ffn_W2"]])
    ar["moe0"] = cc(_np.concatenate([w1[:, :P], w3[:, :P], w1[:, P:], w3[:, P:], w2], axis=2))
    ar["w1"], ar["w2"], ar["b2"] = (cc(g["L1_ffn_" + k]) for k in ("W1", "W2", "b2"))
    ar["b2row"] = ar["b2"].reshape(1, E1 * D)
    ar["b1"] = cc(g["L1_ffn_b1"].reshape(E1, HC, P).transpose(2, 0, 1))
    cf = _np.zeros((P, CF_TOTAL), _np.float32)
    cf[:, 0:128] = _np.eye(P)
    for v in range(4):
        cf[:, CF["vmask"] + v] = (_np.arange(P) // HD) % 4 == v
    cf[:, CF["iota"]:CF["iota"] + 128] = _np.arange(128)
    cf[:, CF["blk"]:CF["blk"] + 16] = _np.arange(16)
    cf[:, CF["power"]:] = -0.5
    ar["cf"] = cf
    cb = _np.zeros((P, CB_TOTAL), _np.float32)
    cb[:, 0:128] = _np.eye(P)
    q, k = _np.arange(P) % T, _np.arange(T)
    cb[:, CB["mask"]:CB["mask"] + 512] = _np.tile(_np.where(k[None] > q[:, None], NEG, 0.0), (1, 8))
    cb[:, CB["upper"]:CB["upper"] + 128] = _np.arange(P)[:, None] < _np.arange(P)[None]
    cb[:, CB["ones"]:CB["ones"] + 128] = 1
    ar["cb"] = cb.astype(bf)

    nc = _bacc.Bacc("TRN2", target_bir_lowering=False, num_devices=1)
    aps = {k: nc.dram_tensor("in_" + k, v.shape, mybir.dt.from_np(v.dtype), kind="ExternalInput").ap() for k, v in ar.items()}
    out = nc.dram_tensor("out_0", (TOK, D), F32, kind="ExternalOutput").ap()
    sx = nc.dram_tensor("slots_x", (NBLK * P, D), F32, kind="Internal").ap()
    sy = nc.dram_tensor("slots_y", (NBLK * P, D), F32, kind="Internal").ap()
    sg = nc.dram_tensor("gates", (E0, TOK), F32, kind="Internal").ap()
    build(nc, aps, out, sx, sy, sg)
    r = _run(nc, [{"in_" + k: v for k, v in ar.items()}], core_ids=[0])
    return r.results[0]["out_0"].reshape(NB, T, D)
```
